# Optimizing a Trainium2 kernel written in Bass

```python
import numpy as np
import jax
import jax.numpy as jnp

def _softmax(x, axis=-1):
    return jax.nn.softmax(x, axis=axis)

def _gelu(x):
    return jax.nn.gelu(x, approximate=True)

def _silu(x):
    return jax.nn.silu(x)

def _sigmoid(x):
    return jax.nn.sigmoid(x)

def _layernorm(x, axis=-1, eps=1e-05):
    m = jnp.mean(x, axis=axis, keepdims=True)
    v = jnp.var(x, axis=axis, keepdims=True)
    return (x - m) / jnp.sqrt(v + eps)

def _scatter_add(tgt, idx, src, axis=0):
    return tgt.at[idx].add(src)

def _segment_sum(src, seg, n):
    return jax.ops.segment_sum(src, seg, n)
kernel_name = 'mk_lm_tower_d1_tok_ids512_r4_524c9d'

def setup_inputs(seed: int=0):
    np.random.seed(seed)
    _w = jnp.asarray

    def _rec_inputs():
        import jax
        import jax.numpy as jnp
        _rk = jax.random.key(seed)
        x = jax.random.randint(jax.random.fold_in(_rk, 1), (128, 128), 0, 31999, jnp.int32)
        return x
    x = _rec_inputs()

    def _L0_tok_setup():
        import jax, jax.numpy as jnp
        import numpy as np
        D_MODEL = 128
        HEADS = 8
        DFF = 512
        LAYERS = 4
        VOCAB = 8000
        MAX_LEN = 1024
        BATCH = 4
        SEQ = 1024
        EPS_LN = 0.001
        EPS_ATTN = 1e-06

        def positional_encoding(length, depth):
            half = depth // 2
            positions = np.arange(length)[:, None]
            depths = np.arange(half)[None, :] / half
            angle_rads = positions * (1.0 / 10000.0 ** depths)
            pe = np.concatenate([np.sin(angle_rads), np.cos(angle_rads)], axis=-1)
            return jnp.asarray(pe, dtype=jnp.float32)

        def _layer_norm(x, g, b):
            m = jnp.mean(x, axis=-1, keepdims=True)
            v = jnp.mean(jnp.square(x - m), axis=-1, keepdims=True)
            return (x - m) * jax.lax.rsqrt(v + EPS_LN) * g + b

        def _encoder_forward(tokens, emb, pos_enc, Wq, bq, Wk, bk, Wv, bv, Wo, bo, ln1_g, ln1_b, W1, b1, W2, b2, ln2_g, ln2_b):
            B, S = tokens.shape
            x = emb[tokens] * jnp.sqrt(jnp.float32(D_MODEL)) + pos_enc[None, :S, :]
            for i in range(LAYERS):
                q = jax.nn.elu((x @ Wq[i] + bq[i]).reshape(B, S, HEADS, -1)) + 1.0
                k = jax.nn.elu((x @ Wk[i] + bk[i]).reshape(B, S, HEADS, -1)) + 1.0
                v = (x @ Wv[i] + bv[i]).reshape(B, S, HEADS, -1)
                key_sum = jnp.sum(k, axis=-1, keepdims=True)
                weighted = jnp.sum(k * v, axis=-1, keepdims=True)
                ctx = q * weighted / (q * key_sum + EPS_ATTN)
                attn = ctx.reshape(B, S, D_MODEL) @ Wo[i] + bo[i]
                x = _layer_norm(x + attn, ln1_g[i], ln1_b[i])
                h = jax.nn.relu(x @ W1[i] + b1[i]) @ W2[i] + b2[i]
                x = _layer_norm(x + h, ln2_g[i], ln2_b[i])
            return x
        key = jax.random.key(seed)
        ks = jax.random.split(key, 8)
        s = 0.02
        L, d = (LAYERS, D_MODEL)
        w = lambda k, shape: jax.random.normal(k, shape, jnp.float32) * s
        return {'tokens': jax.random.randint(ks[0], (BATCH, SEQ), 0, VOCAB), 'emb': w(ks[1], (VOCAB, d)), 'pos_enc': positional_encoding(MAX_LEN + 2, d), 'Wq': w(ks[2], (L, d, d)), 'bq': jnp.zeros((L, d), jnp.float32), 'Wk': w(ks[3], (L, d, d)), 'bk': jnp.zeros((L, d), jnp.float32), 'Wv': w(ks[4], (L, d, d)), 'bv': jnp.zeros((L, d), jnp.float32), 'Wo': w(ks[5], (L, d, d)), 'bo': jnp.zeros((L, d), jnp.float32), 'ln1_g': jnp.ones((L, d), jnp.float32), 'ln1_b': jnp.zeros((L, d), jnp.float32), 'W1': w(ks[6], (L, d, DFF)), 'b1': jnp.zeros((L, DFF), jnp.float32), 'W2': w(ks[7], (L, DFF, d)), 'b2': jnp.zeros((L, d), jnp.float32), 'ln2_g': jnp.ones((L, d), jnp.float32), 'ln2_b': jnp.zeros((L, d), jnp.float32)}
    _L0_tok_all = _L0_tok_setup()
    _L0_tok_in = {k: v for k, v in _L0_tok_all.items() if k in ('emb', 'pos_enc', 'Wq', 'bq', 'Wk', 'bk', 'Wv', 'bv', 'Wo', 'bo', 'ln1_g', 'ln1_b', 'W1', 'b1', 'W2', 'b2', 'ln2_g', 'ln2_b')}
    del _L0_tok_all

    def _L0_attn_setup():
        import jax, jax.numpy as jnp
        import numpy as np
        D = 128
        H = 4
        DK = D // 2
        DV = D
        HK = DK // H
        HV = DV // H
        GATE_LOW_RANK = 16
        GATE_LOGIT_NORMALIZER = 16.0
        LN_EPS = 1e-05

        def _gla(x, Wq, Wk, Wv, Wg, Wgk1, Wgk2, bgk2, Wo):
            B, S, _ = x.shape
            q = (x @ Wq).reshape(B, S, H, HK) * HK ** (-0.5)
            k = (x @ Wk).reshape(B, S, H, HK)
            v = (x @ Wv).reshape(B, S, H, HV)
            g = (x @ Wg).reshape(B, S, H, HV)
            gk = jax.nn.log_sigmoid(x @ Wgk1 @ Wgk2 + bgk2) / GATE_LOGIT_NORMALIZER
            gk = gk.reshape(B, S, H, HK)

            def step(h, inp):
                q_t, k_t, v_t, gk_t = inp
                h = jnp.exp(gk_t)[..., None] * h + k_t[..., None] * v_t[..., None, :]
                o_t = jnp.einsum('bhk,bhkv->bhv', q_t, h)
                return (h, o_t)
            h0 = jnp.zeros((B, H, HK, HV), x.dtype)
            xs = (q.swapaxes(0, 1), k.swapaxes(0, 1), v.swapaxes(0, 1), gk.swapaxes(0, 1))
            _, o = jax.lax.scan(step, h0, xs)
            o = o.swapaxes(0, 1)
            mu = o.mean(-1, keepdims=True)
            var = ((o - mu) ** 2).mean(-1, keepdims=True)
            o = (o - mu) * jax.lax.rsqrt(var + LN_EPS)
            o = o * jax.nn.silu(g)
            return o.reshape(B, S, DV) @ Wo
        key = jax.random.key(seed)
        ks = jax.random.split(key, 9)
        B, S = (2, 4096)
        g = lambda k, shape, scale: jax.random.normal(k, shape, dtype=jnp.float32) * scale
        return {'x': g(ks[0], (B, S, D), 1.0), 'Wq': g(ks[1], (D, DK), D ** (-0.5)), 'Wk': g(ks[2], (D, DK), D ** (-0.5)), 'Wv': g(ks[3], (D, DV), D ** (-0.5)), 'Wg': g(ks[4], (D, DV), D ** (-0.5)), 'Wgk1': g(ks[5], (D, GATE_LOW_RANK), D ** (-0.5)), 'Wgk2': g(ks[6], (GATE_LOW_RANK, DK), GATE_LOW_RANK ** (-0.5)), 'bgk2': jnp.zeros((DK,), jnp.float32), 'Wo': g(ks[7], (DV, D), DV ** (-0.5))}
    _L0_attn_all = _L0_attn_setup()
    _L0_attn_in = {k: v for k, v in _L0_attn_all.items() if k in ('Wq', 'Wk', 'Wv', 'Wg', 'Wgk1', 'Wgk2', 'bgk2', 'Wo')}
    del _L0_attn_all

    def _L0_ffn_setup():
        import jax, jax.numpy as jnp
        import numpy as np
        CAPACITY_FACTOR = 1.2
        key = jax.random.key(seed)
        k1, k2, k3 = jax.random.split(key, 3)
        B, S, D, E = (8, 1024, 128, 16)
        x = jax.random.normal(k1, (B, S, D), dtype=jnp.float32)
        switch_w = jax.random.normal(k2, (E, D), dtype=jnp.float32) * 0.02
        switch_b = jnp.zeros((E,), dtype=jnp.float32)
        expert_w = jax.random.normal(k3, (E, D, D), dtype=jnp.float32) * 0.02
        expert_b = jnp.zeros((E, D), dtype=jnp.float32)
        return {'x': x, 'switch_w': switch_w, 'switch_b': switch_b, 'expert_w': expert_w, 'expert_b': expert_b}
    _L0_ffn_all = _L0_ffn_setup()
    _L0_ffn_in = {k: v for k, v in _L0_ffn_all.items() if k in ('switch_w', 'switch_b', 'expert_w', 'expert_b')}
    del _L0_ffn_all
    return {'x': x, 'L0_tok_emb': _L0_tok_in['emb'], 'L0_tok_pos_enc': _L0_tok_in['pos_enc'], 'L0_tok_Wq': _L0_tok_in['Wq'], 'L0_tok_bq': _L0_tok_in['bq'], 'L0_tok_Wk': _L0_tok_in['Wk'], 'L0_tok_bk': _L0_tok_in['bk'], 'L0_tok_Wv': _L0_tok_in['Wv'], 'L0_tok_bv': _L0_tok_in['bv'], 'L0_tok_Wo': _L0_tok_in['Wo'], 'L0_tok_bo': _L0_tok_in['bo'], 'L0_tok_ln1_g': _L0_tok_in['ln1_g'], 'L0_tok_ln1_b': _L0_tok_in['ln1_b'], 'L0_tok_W1': _L0_tok_in['W1'], 'L0_tok_b1': _L0_tok_in['b1'], 'L0_tok_W2': _L0_tok_in['W2'], 'L0_tok_b2': _L0_tok_in['b2'], 'L0_tok_ln2_g': _L0_tok_in['ln2_g'], 'L0_tok_ln2_b': _L0_tok_in['ln2_b'], 'L0_attn_Wq': _L0_attn_in['Wq'], 'L0_attn_Wk': _L0_attn_in['Wk'], 'L0_attn_Wv': _L0_attn_in['Wv'], 'L0_attn_Wg': _L0_attn_in['Wg'], 'L0_attn_Wgk1': _L0_attn_in['Wgk1'], 'L0_attn_Wgk2': _L0_attn_in['Wgk2'], 'L0_attn_bgk2': _L0_attn_in['bgk2'], 'L0_attn_Wo': _L0_attn_in['Wo'], 'L0_ffn_switch_w': _L0_ffn_in['switch_w'], 'L0_ffn_switch_b': _L0_ffn_in['switch_b'], 'L0_ffn_expert_w': _L0_ffn_in['expert_w'], 'L0_ffn_expert_b': _L0_ffn_in['expert_b']}

def reference(x, L0_tok_emb, L0_tok_pos_enc, L0_tok_Wq, L0_tok_bq, L0_tok_Wk, L0_tok_bk, L0_tok_Wv, L0_tok_bv, L0_tok_Wo, L0_tok_bo, L0_tok_ln1_g, L0_tok_ln1_b, L0_tok_W1, L0_tok_b1, L0_tok_W2, L0_tok_b2, L0_tok_ln2_g, L0_tok_ln2_b, L0_attn_Wq, L0_attn_Wk, L0_attn_Wv, L0_attn_Wg, L0_attn_Wgk1, L0_attn_Wgk2, L0_attn_bgk2, L0_attn_Wo, L0_ffn_switch_w, L0_ffn_switch_b, L0_ffn_expert_w, L0_ffn_expert_b):
    import jax
    import jax.numpy as jnp

    def _L0_tok_ref(tokens, emb, pos_enc, Wq, bq, Wk, bk, Wv, bv, Wo, bo, ln1_g, ln1_b, W1, b1, W2, b2, ln2_g, ln2_b):
        import jax, jax.numpy as jnp
        import numpy as np
        D_MODEL = 128
        HEADS = 8
        DFF = 512
        LAYERS = 4
        VOCAB = 8000
        MAX_LEN = 1024
        BATCH = 4
        SEQ = 1024
        EPS_LN = 0.001
        EPS_ATTN = 1e-06

        def positional_encoding(length, depth):
            half = depth // 2
            positions = np.arange(length)[:, None]
            depths = np.arange(half)[None, :] / half
            angle_rads = positions * (1.0 / 10000.0 ** depths)
            pe = np.concatenate([np.sin(angle_rads), np.cos(angle_rads)], axis=-1)
            return jnp.asarray(pe, dtype=jnp.float32)

        def _layer_norm(x, g, b):
            m = jnp.mean(x, axis=-1, keepdims=True)
            v = jnp.mean(jnp.square(x - m), axis=-1, keepdims=True)
            return (x - m) * jax.lax.rsqrt(v + EPS_LN) * g + b

        def _encoder_forward(tokens, emb, pos_enc, Wq, bq, Wk, bk, Wv, bv, Wo, bo, ln1_g, ln1_b, W1, b1, W2, b2, ln2_g, ln2_b):
            B, S = tokens.shape
            x = emb[tokens] * jnp.sqrt(jnp.float32(D_MODEL)) + pos_enc[None, :S, :]
            for i in range(LAYERS):
                q = jax.nn.elu((x @ Wq[i] + bq[i]).reshape(B, S, HEADS, -1)) + 1.0
                k = jax.nn.elu((x @ Wk[i] + bk[i]).reshape(B, S, HEADS, -1)) + 1.0
                v = (x @ Wv[i] + bv[i]).reshape(B, S, HEADS, -1)
                key_sum = jnp.sum(k, axis=-1, keepdims=True)
                weighted = jnp.sum(k * v, axis=-1, keepdims=True)
                ctx = q * weighted / (q * key_sum + EPS_ATTN)
                attn = ctx.reshape(B, S, D_MODEL) @ Wo[i] + bo[i]
                x = _layer_norm(x + attn, ln1_g[i], ln1_b[i])
                h = jax.nn.relu(x @ W1[i] + b1[i]) @ W2[i] + b2[i]
                x = _layer_norm(x + h, ln2_g[i], ln2_b[i])
            return x
        return _encoder_forward(tokens, emb, pos_enc, Wq, bq, Wk, bk, Wv, bv, Wo, bo, ln1_g, ln1_b, W1, b1, W2, b2, ln2_g, ln2_b)

    def _L0_attn_ref(x, Wq, Wk, Wv, Wg, Wgk1, Wgk2, bgk2, Wo):
        import jax, jax.numpy as jnp
        import numpy as np
        D = 128
        H = 4
        DK = D // 2
        DV = D
        HK = DK // H
        HV = DV // H
        GATE_LOW_RANK = 16
        GATE_LOGIT_NORMALIZER = 16.0
        LN_EPS = 1e-05

        def _gla(x, Wq, Wk, Wv, Wg, Wgk1, Wgk2, bgk2, Wo):
            B, S, _ = x.shape
            q = (x @ Wq).reshape(B, S, H, HK) * HK ** (-0.5)
            k = (x @ Wk).reshape(B, S, H, HK)
            v = (x @ Wv).reshape(B, S, H, HV)
            g = (x @ Wg).reshape(B, S, H, HV)
            gk = jax.nn.log_sigmoid(x @ Wgk1 @ Wgk2 + bgk2) / GATE_LOGIT_NORMALIZER
            gk = gk.reshape(B, S, H, HK)

            def step(h, inp):
                q_t, k_t, v_t, gk_t = inp
                h = jnp.exp(gk_t)[..., None] * h + k_t[..., None] * v_t[..., None, :]
                o_t = jnp.einsum('bhk,bhkv->bhv', q_t, h)
                return (h, o_t)
            h0 = jnp.zeros((B, H, HK, HV), x.dtype)
            xs = (q.swapaxes(0, 1), k.swapaxes(0, 1), v.swapaxes(0, 1), gk.swapaxes(0, 1))
            _, o = jax.lax.scan(step, h0, xs)
            o = o.swapaxes(0, 1)
            mu = o.mean(-1, keepdims=True)
            var = ((o - mu) ** 2).mean(-1, keepdims=True)
            o = (o - mu) * jax.lax.rsqrt(var + LN_EPS)
            o = o * jax.nn.silu(g)
            return o.reshape(B, S, DV) @ Wo
        return _gla(x, Wq, Wk, Wv, Wg, Wgk1, Wgk2, bgk2, Wo)

    def _L0_ffn_ref(x, switch_w, switch_b, expert_w, expert_b):
        import jax, jax.numpy as jnp
        import numpy as np
        CAPACITY_FACTOR = 1.2
        B, S, D = x.shape
        E = switch_w.shape[0]
        N = B * S
        xf = x.reshape(N, D)
        logits = xf @ switch_w.T + switch_b
        probs = jax.nn.softmax(logits, axis=-1)
        route_probs = jnp.max(probs, axis=-1)
        routes = jnp.argmax(probs, axis=-1)
        oh = jax.nn.one_hot(routes, E, dtype=jnp.int32)
        pos = jnp.take_along_axis(jnp.cumsum(oh, axis=0), routes[:, None], axis=1)[:, 0] - 1
        capacity = int(CAPACITY_FACTOR * N / E)
        keep = pos < capacity
        buf = jnp.zeros((E, capacity, D), dtype=xf.dtype).at[routes, pos].set(xf)
        y = jnp.einsum('ecd,efd->ecf', buf, expert_w) + expert_b[:, None, :]
        gathered = y[routes, jnp.minimum(pos, capacity - 1)]
        out = jnp.where(keep[:, None], gathered, xf) * route_probs[:, None]
        return out.reshape(B, S, D)
    h = _L0_tok_ref(x, L0_tok_emb, L0_tok_pos_enc, L0_tok_Wq, L0_tok_bq, L0_tok_Wk, L0_tok_bk, L0_tok_Wv, L0_tok_bv, L0_tok_Wo, L0_tok_bo, L0_tok_ln1_g, L0_tok_ln1_b, L0_tok_W1, L0_tok_b1, L0_tok_W2, L0_tok_b2, L0_tok_ln2_g, L0_tok_ln2_b)
    h = h + _L0_attn_ref(_layernorm(h, axis=-1), L0_attn_Wq, L0_attn_Wk, L0_attn_Wv, L0_attn_Wg, L0_attn_Wgk1, L0_attn_Wgk2, L0_attn_bgk2, L0_attn_Wo)
    h = h + _L0_ffn_ref(_layernorm(h, axis=-1), L0_ffn_switch_w, L0_ffn_switch_b, L0_ffn_expert_w, L0_ffn_expert_b)
    return h

_drawn_inputs = setup_inputs


def setup_inputs(seed=0):
    import zlib

    import numpy as np

    out = dict(_drawn_inputs(seed))
    spreads = {'L0_tok_bq': (0.0, 2.0),
     'L0_tok_bk': (0.0, 0.8),
     'L0_tok_bv': (0.0, 0.48),
     'L0_tok_bo': (0.0, 0.1),
     'L0_tok_ln1_g': (1.0, 0.2),
     'L0_tok_ln1_b': (0.0, 0.1),
     'L0_tok_b1': (0.0, 0.1),
     'L0_tok_b2': (0.0, 0.1),
     'L0_tok_ln2_g': (1.0, 0.2),
     'L0_tok_ln2_b': (0.0, 0.1),
     'L0_attn_bgk2': (0.0, 0.305),
     'L0_ffn_switch_b': (0.0, 0.1),
     'L0_ffn_expert_b': (0.0, 0.8)}
    factors = {'L0_tok_Wq': 64.0, 'L0_tok_Wk': 6.337, 'L0_ffn_expert_w': 4.703}
    for name, (base, spread) in spreads.items():
        noise = np.random.default_rng([zlib.crc32(name.encode()), seed]).standard_normal(out[name].shape)
        drawn = base * np.exp(spread * noise) if base else spread * noise
        out[name] = jnp.asarray(drawn.astype(out[name].dtype))
    for name, factor in factors.items():
        out[name] = (out[name] * factor).astype(out[name].dtype)
    return out
```

```python
from contextlib import ExitStack

import concourse.bass as bass
from concourse import mybir

F32 = mybir.dt.float32
BF16 = mybir.dt.bfloat16
I32 = mybir.dt.int32
U32 = mybir.dt.uint32
ALU = mybir.AluOpType
ACT = mybir.ActivationFunctionType
AX_X = mybir.AxisListType.X

P = 128
D = 128
LAYERS = 4
HEAD = 16
DFF = 512
FB = DFF // P
S = 128
SEQS = 4
TILE = SEQS * S
STREAMS = 2
GH = 4
GK = 16
GV = 32
HALF = S // 2
E = 16
ROW = D + 4
CHUNKS = 10
SLOTS = CHUNKS * P
FAR = 1.0e6
DECAY_MAX = 960.0
LAG = 14

VEC = ["bq", "bk", "bv", "bo", "ln1_g", "ln1_b", "b2", "ln2_g", "ln2_b", "b1_0", "b1_1", "b1_2", "b1_3"]
NV = len(VEC)

STAGES = ["embed"]
for _l in range(LAYERS):
    STAGES += [(n, _l) for n in ("qkv", "sums", "mix", "var1", "up", "down", "var2")]
STAGES += ["centre", "cvar", "gates", "values", "decay", "scores", "outs", "ovar", "project", "stats", "route", "slots"]


def stage_order(it, before=None):
    n = len(STAGES)
    for i in range(n):
        yield it, 0, STAGES[i]
        if i >= LAG:
            yield it, 1, STAGES[i - LAG]
        elif before is not None:
            yield before, 1, STAGES[n - LAG + i]


def last_stages(it):
    for name in STAGES[len(STAGES) - LAG:]:
        yield it, 1, name


def build(nc, tok, emb, pos, wq, wk, wv, wo, w1, w2, vec, gq, gk, gv, gg, gk1_t, gk2, gb, go, go_t, sw, sb, ew, eb, out):
    VOCAB = emb.shape[0]
    B = tok.shape[1]
    N = B * S
    TILES = B // SEQS
    PAIRS = TILES // STREAMS
    CAP = int(1.2 * N / E)
    assert CAP <= SLOTS and E * SLOTS < FAR and N < FAR

    with ExitStack() as ctx:
        def sbuf(name, shape, dt=F32):
            return ctx.enter_context(nc.sbuf_tensor(name, shape, dt))

        def sem(name):
            return ctx.enter_context(nc.semaphore(name))

        slots_dram = nc.dram_tensor("slot_rows", (E * SLOTS, ROW), F32, kind="Internal").ap()

        ident = sbuf("ident", [P, P])
        centre = sbuf("centre", [P, P])
        mean_all = sbuf("mean_all", [P, P])
        head_sum = sbuf("head_sum", [P, P])
        mean_v = sbuf("mean_v", [P, P])
        causal = sbuf("causal", [P, P])
        tri = sbuf("tri", [P, P], BF16)
        ones_b = sbuf("ones_b", [P, P], BF16)
        ones_r = sbuf("ones_r", [1, P])
        onesf = sbuf("onesf", [P, P])
        restart = sbuf("restart", [P, SEQS, S])
        eps_attn = sbuf("eps_attn", [P, 1])
        eps_tower = sbuf("eps_tower", [P, 1])
        eps_norm = sbuf("eps_norm", [P, 1])
        one_c = sbuf("one_c", [P, 1])
        half_i = sbuf("half_i", [P, 1], I32)
        half_f = sbuf("half_f", [P, 1])
        half_sel = sbuf("half_sel", [P, 2])
        half_scale = sbuf("half_scale", [P, 2])
        rank = sbuf("rank", [P, SEQS, E])
        token_no = sbuf("token_no", [P, SEQS])
        void_row = sbuf("void_row", [P, ROW])

        vecs = sbuf("vecs", [P, LAYERS * NV])
        zcol = sbuf("zcol", [P, 6, LAYERS])
        zb1 = sbuf("zb1", [P, LAYERS, FB])
        zmix = sbuf("zmix", [P, LAYERS])
        zdown = sbuf("zdown", [P, LAYERS])
        zcen = sbuf("zcen", [P, 1])
        work = sbuf("work", [P, LAYERS, 2])
        wqs = sbuf("wqs", [P, LAYERS, D])
        wks = sbuf("wks", [P, LAYERS, D])
        wvs = sbuf("wvs", [P, LAYERS, D])
        wos = sbuf("wos", [P, LAYERS, D])
        w1s = sbuf("w1s", [P, LAYERS, DFF])
        w2s = sbuf("w2s", [P, LAYERS, FB, D])
        wmean = sbuf("wmean", [P, LAYERS * (FB + 1) + GH])
        res1 = sbuf("res1", [P, LAYERS, D])
        res2 = sbuf("res2", [P, LAYERS, D])
        res3 = sbuf("res3", [P, D])
        gqs = sbuf("gqs", [P, P])
        gks = sbuf("gks", [P, P])
        gvs = sbuf("gvs", [P, D])
        ggs = sbuf("ggs", [P, D])
        gk1s = sbuf("gk1s", [GK, P])
        gk2s = sbuf("gk2s", [GK, P])
        gates_w = sbuf("gates_w", [P, P])
        gbs = sbuf("gbs", [P, 1])
        goT = sbuf("goT", [P, D])
        sws = sbuf("sws", [P, E])
        csw = sbuf("csw", [P, E])
        out_w = sbuf("out_w", [P, D + E])
        res_w = sbuf("res_w", [P, D + E])
        sbs = sbuf("sbs", [P, E])
        ews = sbuf("ews", [P, E, D])
        ebs = sbuf("ebs", [1, E, D])
        posT = sbuf("posT", [P, S])

        def per_stream(name, shape, dt=F32):
            return [sbuf(f"{name}{s}", shape, dt) for s in range(STREAMS)]

        ids = sbuf("ids", [P, B], I32)
        id_wrap = sbuf("id_wrap", [P, B])
        id_float = sbuf("id_float", [P, B])
        id_row = sbuf("id_row", [P, B + STREAMS * SEQS], U32)
        idx = per_stream("idx", [P, SEQS], U32)
        rows = per_stream("rows", [P, SEQS, D])
        x = per_stream("x", [P, TILE])
        eq = per_stream("eq", [P, TILE])
        ek = per_stream("ek", [P, TILE])
        qf = per_stream("qf", [P, TILE])
        kf = per_stream("kf", [P, TILE])
        kv = per_stream("kv", [P, TILE])
        t = per_stream("t", [P, TILE])
        u = per_stream("u", [P, TILE])
        cx = per_stream("cx", [P, TILE])
        sq = per_stream("sq", [P, TILE])
        rs = per_stream("rs", [P, TILE])
        n1 = per_stream("n1", [P, TILE])
        hid = per_stream("hid", [P, FB, TILE])
        hT = per_stream("hT", [P, TILE])
        row = per_stream("row", [P, SEQS, ROW])
        plain = per_stream("plain", [P, SEQS, D])
        st = per_stream("st", [P, SEQS, 6])
        mv = per_stream("mv", [P, SEQS, 2])
        lnv = per_stream("lnv", [P, SEQS])
        sc1 = per_stream("sc1", [P, SEQS])
        sc2 = per_stream("sc2", [P, SEQS])
        sc3 = per_stream("sc3", [P, SEQS])
        ref = per_stream("ref", [P, SEQS])
        ref_a = per_stream("ref_a", [P, SEQS])
        lg = per_stream("lg", [P, SEQS, E])
        lgm = per_stream("lgm", [P, SEQS, E])
        ex = per_stream("ex", [P, SEQS, E])
        cand = per_stream("cand", [P, SEQS, E])
        oh = per_stream("oh", [P, SEQS, E])
        ohb = per_stream("ohb", [P, SEQS, E], BF16)
        mx = per_stream("mx", [P, SEQS])
        m2 = per_stream("m2", [P, SEQS])
        sm = per_stream("sm", [P, SEQS])
        place = per_stream("place", [P, SEQS])
        over = per_stream("over", [P, SEQS])
        pick = per_stream("pick", [P, SEQS, E])
        slot_f = per_stream("slot_f", [P, SEQS])
        slot = per_stream("slot", [P, SEQS], U32)
        before = sbuf("before", [P, STREAMS * SEQS + 1, E])

        banks = [[ctx.enter_context(nc.psum_tensor(f"bank{s}{i}", [P, 512], F32)) for i in range(4)]
                 for s in range(STREAMS)]

        mn, lsp, G, dG, eQ, eK = eq, ek, t, u, qf, kf
        Q, K, V, gsil = cx, sq, eq, x

        load_w = sem("load_w")
        const = sem("const")
        const2 = sem("const2")
        prep_pe = sem("prep_pe")
        prep_dve = sem("prep_dve")
        ready = sem("ready")
        void_out = sem("void_out")

        def each(name):
            return [sem(f"{name}{s}") for s in range(STREAMS)]

        idx_done = each("idx_done")
        rows_in = each("rows_in")
        embT = each("embT")
        x0 = each("x0")
        s_qkv = each("s_qkv")
        s_exp = each("s_exp")
        s_min = each("s_min")
        s_elu = each("s_elu")
        s_kv = each("s_kv")
        s_sum = each("s_sum")
        s_tu = each("s_tu")
        s_rcp = each("s_rcp")
        s_cx = each("s_cx")
        s_z = each("s_z")
        s_sq = each("s_sq")
        s_var = each("s_var")
        s_rs = each("s_rs")
        s_y = each("s_y")
        s_h = each("s_h")
        s_relu = [each("s_relu_act"), each("s_relu_dve")]
        g_hT = each("g_hT")
        g_proj = each("g_proj")
        g_act = each("g_act")
        g_dve = each("g_dve")
        g_pool = each("g_pool")
        g_score = each("g_score")
        g_mask = each("g_mask")
        g_o = each("g_o")
        g_h2 = each("g_h2")
        r_act = each("r_act")
        r_dve = each("r_dve")
        r_cnt = each("r_cnt")
        row_out = each("row_out")
        plain_out = each("plain_out")

        f_in = [sem("f_in0"), sem("f_in1")]
        f_xf = sem("f_xf")
        f_tr = sem("f_tr")
        f_xT = sem("f_xT")
        f_y = sem("f_y")
        f_o = sem("f_o")
        f_id = sem("f_id")
        f_out = [sem("f_out0"), sem("f_out1")]

        pool_step = sem("pool_step")
        rank_i = sbuf("rank_i", [P, SEQS, E], I32)
        token_i = sbuf("token_i", [P, SEQS], I32)
        prep_v = sem("prep_v")
        row_free = each("row_free")
        plain_free = each("plain_free")
        f_free = [sem("f_free0"), sem("f_free1")]
        r_before = sem("r_before")
        r_slot = each("r_slot")
        void_col = sbuf("void_col", [P, 1])
        tile_start = [sbuf(f"tile_start{s}", [P, 1]) for s in range(STREAMS)]
        R_BEF = STREAMS * SEQS + 1
        ftr = banks[0]
        fyb = banks[1]
        xfT = [t[0], u[0], cx[0], sq[0]]
        zero_col = sbuf("zero_col", [P, 1])
        xin = [sbuf("xin0", [P, CHUNKS, ROW]), sbuf("xin1", [P, CHUNKS, ROW])]
        xfn = [eq[0], ek[0], qf[0], kf[0]]
        idp = [sbuf("idp0", [P, CHUNKS], U32), sbuf("idp1", [P, CHUNKS], U32)]
        yo = [sbuf("yo0", [P, CHUNKS, D]), sbuf("yo1", [P, CHUNKS, D])]
        NG_ACT = 12
        NG_DVE = 13
        R_ACT = 8
        R_DVE = 19

        WLOADS = 32
        block = ctx.enter_context(nc.Block())

        PER_Y = 2 * LAYERS + 1

        def slot_rows(e):
            return slots_dram[bass.ds(e * SLOTS, SLOTS), :].rearrange("(p c) r -> p c r", p=P)

        alone = {e: sem(f"alone_{e}") for e in ("pool", "dve")}

        def wait_alone(eng, s, value):
            eng.wait_ge(s, value)
            eng.sem_inc(alone["pool" if eng.engine == nc.gpsimd.engine else "dve"], 1)

        @block.sync
        def _(sp):
            loads = [
                (vecs[:], vec), (posT[:], pos), (wqs[:], wq.rearrange("l i o -> i l o")),
                (wks[:], wk.rearrange("l i o -> i l o")), (wvs[:], wv.rearrange("l i o -> i l o")),
                (wos[:], wo.rearrange("l i o -> i l o")), (w1s[:], w1.rearrange("l i o -> i l o")),
                (w2s[:], w2.rearrange("l (j i) o -> i l j o", i=P)),
                (gvs[:], gv), (ggs[:], gg), (gk1s[:], gk1_t), (out_w[:, 0:D], go), (sws[:], sw), (ews[:], ew), (ids[:], tok),
                (ebs[:], eb), (sbs[:], sb.partition_broadcast(P)), (goT[:], go_t),
            ]
            with nc.allow_non_contiguous_dma("small operands, once"):
                pads = [(gqs, gq), (gks, gk), (gk2s, gk2)]
                sp.wait_ge(const2, 1)
                for dst, src in loads:
                    sp.dma_start(dst, src).then_inc(load_w, 16)
                for f in range(2):
                    for dst, src in pads:
                        sp.dma_start(dst[:].rearrange("p (h f c) -> p f h c", h=GH, f=2)[:, f],
                                     src.rearrange("p (h c) -> p h c", h=GH)).then_inc(load_w, 16)
                    for h in range(GH):
                        sp.dma_start(gbs[32 * h + GK * f:32 * h + GK * (f + 1), :],
                                     gb[h * GK:(h + 1) * GK, :]).then_inc(load_w, 16)
                for c in range(E * CHUNKS // 10):
                    sp.dma_start(slots_dram[c * SLOTS:(c + 1) * SLOTS, :].rearrange("(p c) r -> p c r", p=P),
                                 void_row[:].unsqueeze(1).to_broadcast([P, CHUNKS, ROW])).then_inc(void_out, 16)
            def store_plain(it, s):
                sp.wait_ge(r_act[s], it * R_ACT + R_ACT)
                sp.dma_start(out_tile(it, s), plain[s][:]).then_inc(plain_out[s], 16)

            def out_tile(it, s):
                return out[bass.ds(it * (STREAMS * TILE) + s * TILE, TILE), :].rearrange("(q p) d -> p q d", p=P)

            with sp.Fori(0, PAIRS) as it:
                for s in range(STREAMS):
                    store_plain(it, s)
                for s in range(STREAMS):
                    sp.wait_ge(row_out[s], it * (16 * SEQS) + 16 * SEQS)
                    sp.sem_inc(row_free[s], 1)
                    sp.wait_ge(plain_out[s], it * 16 + 16)
                    sp.sem_inc(plain_free[s], 1)
            for s in range(STREAMS):
                sp.wait_ge(plain_out[s], 16 * PAIRS)
            for s in range(STREAMS):
                sp.wait_ge(row_out[s], 16 * SEQS * PAIRS)
            for b in range(2):
                sp.dma_start(xin[b][:], slot_rows(b)).then_inc(f_in[b], 16)
            with sp.Fori(0, E // 2 - 1) as e2:
                for b in range(2):
                    sp.wait_ge(f_o, e2 * (2 * CHUNKS) + (b + 1) * CHUNKS + 4)
                    sp.wait_ge(f_id, e2 * 2 + b + 1)
                    sp.dma_start(xin[b][:], slot_rows(e2 * 2 + b + 2)).then_inc(f_in[b], 16)
                for b in range(2):
                    sp.wait_ge(f_out[b], e2 * (16 * CHUNKS) + 16 * CHUNKS)
                    sp.sem_inc(f_free[b], 1)
            for b in range(2):
                sp.wait_ge(f_out[b], 16 * CHUNKS * E // 2)



        @block.tensor
        def _(pe):
            pe.wait_ge(load_w, 16 * WLOADS)
            pe.wait_ge(const, 5)
            pe.wait_ge(prep_dve, 1)
            b0, b1_, b2_, b3 = banks[0]
            for l in range(LAYERS):
                v = vecs[:, l * NV:(l + 1) * NV]
                if l > 0:
                    beta = vecs[:, (l - 1) * NV + VEC.index("ln2_b"):(l - 1) * NV + VEC.index("ln2_b") + 1]
                else:
                    beta = zero_col[:]
                for i, w in enumerate((wqs, wks, wvs)):
                    pe.matmul(b0[:, 3 * l + i:3 * l + i + 1], w[:, l, :], beta, start=True, stop=True)
                pe.matmul(b0[:, 16 + l:17 + l], centre[:], work[:, l, 0:1], start=True, stop=True)
                pe.matmul(b0[:, 20 + l:21 + l], centre[:], work[:, l, 1:2], start=True, stop=True)
                g = VEC.index("ln1_b")
                for j in range(FB):
                    pe.matmul(b0[:, 32 + FB * l + j:33 + FB * l + j], w1s[:, l, j * P:(j + 1) * P], v[:, g:g + 1],
                              start=True, stop=True)
            pe.matmul(b0[:, 24:25], centre[:],
                      vecs[:, (LAYERS - 1) * NV + VEC.index("ln2_b"):(LAYERS - 1) * NV + VEC.index("ln2_b") + 1],
                      start=True, stop=True)
            pe.matmul(b1_[:, 0:P], gk1s[:], gk2s[:], start=True, stop=True)
            pe.matmul(b2_[:, 0:E], centre[:], sws[:], start=True, stop=True).then_inc(prep_pe, 1)
            pe.wait_ge(prep_dve, 2)
            pe.matmul(b3[:, 0:E], goT[:], csw[:], start=True, stop=True).then_inc(prep_pe, 1)
            pe.wait_ge(ready, 1)

            def embed(it, s):
                b = banks[s][0]
                pe.wait_ge(rows_in[s], it * (16 * SEQS) + 16 * SEQS)
                for q in range(SEQS):
                    mm = pe.transpose(b[:, q * S:(q + 1) * S], rows[s][:, q, :], ident[:])
                mm.then_inc(embT[s], 1)

            def qkv(it, s, l):
                if l == 0:
                    pe.wait_ge(x0[s], it + 1)
                else:
                    pe.wait_ge(s_y[s], it * PER_Y + 2 * l)
                for b, w in ((1, wks), (0, wqs), (2, wvs)):
                    pe.matmul(banks[s][b][:], w[:, l, :], x[s][:], start=True, stop=True).then_inc(s_qkv[s], 1)

            def sums(it, s, l):
                pe.wait_ge(s_elu[s], it * (2 * LAYERS) + 2 * l + 1)
                pe.matmul(banks[s][3][:], head_sum[:], kf[s][:], start=True, stop=True).then_inc(s_sum[s], 1)
                pe.wait_ge(s_kv[s], it * LAYERS + l + 1)
                pe.matmul(banks[s][1][:], head_sum[:], kv[s][:], start=True, stop=True).then_inc(s_sum[s], 1)

            def mix(it, s, l):
                pe.wait_ge(s_elu[s], it * (2 * LAYERS) + 2 * l + 2)
                pe.matmul(banks[s][0][:], res1[:, l, :], x[s][:], start=True, stop=False)
                pe.wait_ge(s_cx[s], it * LAYERS + l + 1)
                pe.matmul(banks[s][0][:], wos[:, l, :], cx[s][:], start=False, stop=True).then_inc(s_z[s], 1)

            def var(it, s, n, b):
                pe.wait_ge(s_sq[s], it * PER_Y + n + 1)
                pe.matmul(banks[s][b][:], mean_all[:], sq[s][:], start=True, stop=True).then_inc(s_var[s], 1)

            def up(it, s, l):
                pe.wait_ge(s_y[s], it * PER_Y + 2 * l + 1)
                for j, b in enumerate((3, 1, 2, 0)):
                    pe.matmul(banks[s][b][:], w1s[:, l, j * P:(j + 1) * P], n1[s][:], start=True, stop=True) \
                        .then_inc(s_h[s], 1)

            def down(it, s, l):
                for j in range(FB):
                    pe.wait_ge(s_relu[j % 2][s], it * (FB // 2 * LAYERS) + FB // 2 * l + j // 2 + 1)
                    if j == 0:
                        pe.matmul(banks[s][3][:], res2[:, l, :], n1[s][:], start=True, stop=False)
                    mm = pe.matmul(banks[s][3][:], w2s[:, l, j, :], hid[s][:, j, :], start=False, stop=j == FB - 1)
                mm.then_inc(s_z[s], 1)

            def centre_(it, s):
                pe.wait_ge(s_y[s], it * PER_Y + 2 * LAYERS)
                pe.matmul(banks[s][0][:], res3[:], x[s][:], start=True, stop=True).then_inc(s_z[s], 1)

            def gates(it, s):
                pe.wait_ge(s_y[s], it * PER_Y + PER_Y)
                for b, w in enumerate((gates_w, gqs, gks, ggs)):
                    pe.matmul(banks[s][b][:], w[:], hid[s][:, 0, :], start=True, stop=True).then_inc(g_proj[s], 1)

            def values(it, s):
                pe.wait_ge(g_act[s], it * NG_ACT + 1)
                pe.wait_ge(g_dve[s], it * NG_DVE + 1)
                for q in range(SEQS):
                    mm = pe.matmul(banks[s][0][:, q * S:(q + 1) * S], hid[s][:, 0, q * S:(q + 1) * S], gvs[:],
                                   start=True, stop=True)
                mm.then_inc(g_proj[s], 1)

            def scores(it, s):
                pe.wait_ge(g_dve[s], it * NG_DVE + 12)
                pe.wait_ge(g_act[s], it * NG_ACT + 7)
                for h in range(GH):
                    r = slice(32 * h, 32 * h + 32)
                    for q in range(SEQS):
                        c = slice(q * S, (q + 1) * S)
                        mm = pe.matmul(banks[s][h][:, c], K[s][r, c], Q[s][r, c], start=True, stop=True)
                    mm.then_inc(g_score[s], 1)

            def outs(it, s):
                for h in range(GH):
                    pe.wait_ge(g_mask[s], it * GH + h + 1)
                    for q in range(SEQS):
                        mm = pe.matmul(banks[s][0][32 * h:32 * h + 32, q * S:(q + 1) * S],
                                       V[s][:, q * S + 32 * h:q * S + 32 * h + 32],
                                       hid[s][:, h, q * S:(q + 1) * S], start=True, stop=True)
                mm.then_inc(g_o[s], 1)

            def ovar(it, s):
                pe.wait_ge(g_act[s], it * NG_ACT + 10)
                pe.matmul(banks[s][1][:], mean_v[:], sq[s][:], start=True, stop=True).then_inc(g_o[s], 1)

            def project(it, s):
                pe.wait_ge(g_hT[s], it + 1)
                pe.wait_ge(g_pool[s], it + 1)
                for q in range(SEQS):
                    c = slice(q * S, (q + 1) * S)
                    o = banks[s][2 + q // 2][:, (q % 2) * (D + E):(q % 2 + 1) * (D + E)]
                    pe.matmul(o, hT[s][:, c], res_w[:], start=True, stop=False)
                    mm = pe.matmul(o, cx[s][:, c], out_w[:], start=False, stop=True)
                mm.then_inc(g_h2[s], 1)

            def route(it, s):
                pe.wait_ge(r_dve[s], it * R_DVE + 11)
                o = ohb[s][:].rearrange("p q e -> p (q e)")
                pe.matmul(banks[s][1][:, 0:SEQS * E], tri[:], o, start=True, stop=True)
                pe.matmul(banks[s][1][:, SEQS * E:2 * SEQS * E], ones_b[:], o, start=True, stop=True) \
                    .then_inc(r_cnt[s], 1)

            def stage(it, s, name):
                if name == "embed":
                    embed(it, s)
                elif name == "centre":
                    centre_(it, s)
                elif name == "cvar":
                    var(it, s, 2 * LAYERS, 2)
                elif name == "gates":
                    gates(it, s)
                elif name == "values":
                    values(it, s)
                elif name == "scores":
                    scores(it, s)
                elif name == "outs":
                    outs(it, s)
                elif name == "ovar":
                    ovar(it, s)
                elif name == "project":
                    project(it, s)
                elif name == "route":
                    route(it, s)
                elif name[0] == "qkv":
                    qkv(it, s, name[1])
                elif name[0] == "sums":
                    sums(it, s, name[1])
                elif name[0] == "mix":
                    mix(it, s, name[1])
                elif name[0] == "var1":
                    var(it, s, 2 * name[1], 2)
                elif name[0] == "up":
                    up(it, s, name[1])
                elif name[0] == "down":
                    down(it, s, name[1])
                elif name[0] == "var2":
                    var(it, s, 2 * name[1] + 1, 1)

            for at in stage_order(0):
                stage(*at)
            with pe.Fori(0, PAIRS - 1) as j:
                for at in stage_order(j + 1, before=j):
                    stage(*at)
            for at in last_stages(PAIRS - 1):
                stage(*at)

            def expert_chunk(e, c, cc):
                pe.wait_ge(f_xf, e * CHUNKS + c + 1)
                pe.transpose(ftr[cc % 4][:, 0:P], xfn[cc % 4][:, 0:P], ident[:]).then_inc(f_tr, 1)

            def expert_product(e, c, cc):
                pe.wait_ge(f_xT, e * CHUNKS + c + 1)
                pe.wait_ge(f_o, e * CHUNKS + c + 1)
                o = fyb[cc % 4][:, 0:P]
                pe.matmul(o, xfT[cc % 4][:, 0:P], ews[:, bass.ds(e, 1), :].rearrange("p a d -> p (a d)"),
                          start=True, stop=False)
                pe.matmul(o, ones_r[:], ebs[0:1, bass.ds(e, 1), :].rearrange("p a d -> p (a d)"),
                          start=False, stop=True).then_inc(f_y, 1)

            with pe.Fori(0, E // 2) as e2:
                for i in range(2 * CHUNKS + 1):
                    if i < 2 * CHUNKS:
                        expert_chunk(e2 * 2 + i // CHUNKS, i % CHUNKS, i)
                    if i >= 1:
                        expert_product(e2 * 2 + (i - 1) // CHUNKS, (i - 1) % CHUNKS, i - 1)


        @block.scalar
        def _(act):
            act.preload_act_table_set("natural_log_exp_and_others")
            act.wait_ge(ready, 1)

            def qkv(it, s, l):
                act.wait_ge(s_qkv[s], it * (3 * LAYERS) + 3 * l + 1)
                act.activation(ek[s][:], banks[s][1][:], ACT.Exp, bias=zcol[:, 2, l:l + 1]).then_inc(s_exp[s], 1)
                act.wait_ge(s_qkv[s], it * (3 * LAYERS) + 3 * l + 2)
                act.activation(eq[s][:], banks[s][0][:], ACT.Exp, bias=zcol[:, 0, l:l + 1]).then_inc(s_exp[s], 1)

            def sums(it, s, l):
                act.wait_ge(s_tu[s], it * (2 * LAYERS) + 2 * l + 1)
                act.activation(t[s][:], t[s][:], ACT.Ln, bias=eps_attn[:]).then_inc(s_rcp[s], 1)
                act.wait_ge(s_rcp[s], it * (2 * LAYERS) + 2 * l + 1)
                act.activation(t[s][:], t[s][:], ACT.Exp, scale=-1.0).then_inc(s_rcp[s], 1)

            def up(it, s, l):
                for j, b in ((0, 3), (2, 2)):
                    act.wait_ge(s_h[s], it * (FB * LAYERS) + FB * l + j + 1)
                    act.activation(hid[s][:, j, :], banks[s][b][:], ACT.Relu, bias=zb1[:, l, j:j + 1]) \
                        .then_inc(s_relu[0][s], 1)

            def square(it, s, n, b, shift):
                act.wait_ge(s_z[s], it * PER_Y + n + 1)
                act.activation(sq[s][:], banks[s][b][:], ACT.Square, bias=shift).then_inc(s_sq[s], 1)

            def deviation(it, s, n, b, eps):
                act.wait_ge(s_var[s], it * PER_Y + n + 1)
                act.activation(rs[s][:], banks[s][b][:], ACT.Ln, bias=eps[:]).then_inc(s_rs[s], 1)
                act.wait_ge(s_rs[s], it * (2 * PER_Y) + 2 * n + 1)
                act.activation(rs[s][:], rs[s][:], ACT.Exp, scale=-0.5).then_inc(s_rs[s], 1)

            def gates(it, s):
                act.wait_ge(g_proj[s], it * 5 + 1)
                act.activation(lsp[s][:], banks[s][0][:], ACT.Abs, bias=gbs[:]).then_inc(g_act[s], 1)
                act.wait_ge(g_act[s], it * NG_ACT + 1)
                act.activation(lsp[s][:], lsp[s][:], ACT.Exp, scale=-1.0).then_inc(g_act[s], 1)
                act.wait_ge(g_act[s], it * NG_ACT + 2)
                act.activation(lsp[s][:], lsp[s][:], ACT.Ln, bias=one_c[:]).then_inc(g_act[s], 1)
                act.wait_ge(g_dve[s], it * NG_DVE + 2)
                act.activation(hid[s][:, 1, :], hid[s][:, 2, :], ACT.Exp, scale=-1.0).then_inc(g_act[s], 1)
                act.wait_ge(g_act[s], it * NG_ACT + 4)
                act.activation(hid[s][:, 1, :], hid[s][:, 1, :], ACT.Ln, bias=one_c[:]).then_inc(g_act[s], 1)
                act.wait_ge(g_act[s], it * NG_ACT + 5)
                act.activation(hid[s][:, 1, :], hid[s][:, 1, :], ACT.Exp, scale=-1.0).then_inc(g_act[s], 1)

            def values(it, s):
                act.wait_ge(g_proj[s], it * 5 + 5)
                act.wait_ge(g_dve[s], it * NG_DVE + 3)
                act.activation(V[s][:], banks[s][0][:], ACT.Copy).then_inc(g_act[s], 1)

            def decay(it, s):
                act.wait_ge(g_dve[s], it * NG_DVE + 8)
                act.activation(eQ[s][:], dG[s][:], ACT.Exp, scale=1.0 / 16).then_inc(g_act[s], 1)
                act.activation(eK[s][:], dG[s][:], ACT.Exp, scale=-1.0 / 16).then_inc(g_act[s], 1)

            def outs(it, s):
                act.wait_ge(g_o[s], it * 2 + 1)
                act.activation(sq[s][:], banks[s][0][:], ACT.Square).then_inc(g_act[s], 1)

            def ovar(it, s):
                act.wait_ge(g_o[s], it * 2 + 2)
                act.activation(rs[s][:], banks[s][1][:], ACT.Ln, bias=eps_norm[:]).then_inc(g_act[s], 1)
                act.wait_ge(g_act[s], it * NG_ACT + 11)
                act.activation(rs[s][:], rs[s][:], ACT.Exp, scale=-0.5).then_inc(g_act[s], 1)

            def project(it, s):
                act.wait_ge(g_h2[s], it + 1)
                act.wait_ge(row_free[s], it + 1)
                for i in range(2):
                    last = act.activation(row[s][:, 2 * i:2 * i + 2, 0:D],
                                          banks[s][2 + i][:, 0:2 * (D + E)].rearrange("p (q d) -> p q d", q=2)[:, :, 0:D],
                                          ACT.Copy)
                last.then_inc(r_act[s], 1)

            def stats(it, s):
                act.wait_ge(r_dve[s], it * R_DVE + 2)
                act.activation(lnv[s][:], mv[s][:, :, 1], ACT.Ln, bias=eps_norm[:]).then_inc(r_act[s], 1)
                act.wait_ge(r_act[s], it * R_ACT + 2)
                act.activation(row[s][:, :, D + 1], lnv[s][:], ACT.Exp, scale=-0.5).then_inc(r_act[s], 1)

            def route(it, s):
                act.wait_ge(r_dve[s], it * R_DVE + 6)
                act.activation(ex[s][:], lgm[s][:], ACT.Exp).then_inc(r_act[s], 1)

            def slots(it, s):
                act.wait_ge(r_dve[s], it * R_DVE + 17)
                act.wait_ge(plain_free[s], it + 1)
                for q in range(SEQS):
                    act.activation(plain[s][:, q, :], row[s][:, q, 0:D], ACT.Identity, bias=sc3[s][:, q:q + 1],
                                   scale=sc2[s][:, q:q + 1]).then_inc(r_act[s], 1)

            def stage(it, s, name):
                if name == "centre":
                    square(it, s, 2 * LAYERS, 0, zcen[:])
                elif name == "cvar":
                    deviation(it, s, 2 * LAYERS, 2, eps_norm)
                elif name == "gates":
                    gates(it, s)
                elif name == "values":
                    values(it, s)
                elif name == "decay":
                    decay(it, s)
                elif name == "outs":
                    outs(it, s)
                elif name == "ovar":
                    ovar(it, s)
                elif name == "project":
                    project(it, s)
                elif name == "stats":
                    stats(it, s)
                elif name == "route":
                    route(it, s)
                elif name == "slots":
                    slots(it, s)
                elif name[0] == "qkv":
                    qkv(it, s, name[1])
                elif name[0] == "sums":
                    sums(it, s, name[1])
                elif name[0] == "mix":
                    square(it, s, 2 * name[1], 0, zmix[:, name[1]:name[1] + 1])
                elif name[0] == "var1":
                    deviation(it, s, 2 * name[1], 2, eps_tower)
                elif name[0] == "up":
                    up(it, s, name[1])
                elif name[0] == "down":
                    square(it, s, 2 * name[1] + 1, 3, zdown[:, name[1]:name[1] + 1])
                elif name[0] == "var2":
                    deviation(it, s, 2 * name[1] + 1, 1, eps_tower)

            for at in stage_order(0):
                stage(*at)
            with act.Fori(0, PAIRS - 1) as j:
                for at in stage_order(j + 1, before=j):
                    stage(*at)
            for at in last_stages(PAIRS - 1):
                stage(*at)

            with act.Fori(0, E // 2) as e2:
                for i in range(2 * CHUNKS):
                    act.wait_ge(f_tr, e2 * (2 * CHUNKS) + i + 1)
                    act.activation(xfT[i % 4][:, 0:P], ftr[i % 4][:, 0:P], ACT.Copy).then_inc(f_xT, 1)

        @block.vector
        def _(dve):
            dve.memset(zero_col[:], 0.0).then_inc(const, 1)
            dve.wait_ge(load_w, 16 * WLOADS)
            dve.wait_ge(const, 5)

            def col(l, name):
                i = l * NV + VEC.index(name)
                return vecs[:, i:i + 1]

            for l in range(LAYERS):
                beta = col(l - 1, "ln2_b") if l else zero_col[:]
                dve.tensor_tensor(work[:, l, 0:1], col(l, "bo"), beta, ALU.add)
                last = dve.tensor_tensor(work[:, l, 1:2], col(l, "b2"), col(l, "ln1_b"), ALU.add)
            last.then_inc(prep_dve, 1)
            k = 0
            wm = []
            for l in range(LAYERS):
                wm.append((wos[:, l, :], k))
                k += 1
                for j in range(FB):
                    wm.append((w2s[:, l, j, :], k))
                    k += 1
            for h in range(GH):
                wm.append((gvs[:, h * GV:(h + 1) * GV], k))
                k += 1
            for w, i in wm:
                last = dve.tensor_reduce(wmean[:, i:i + 1], w, AX_X, ALU.add)
            last.then_inc(prep_v, 1)
            dve.wait_ge(prep_v, 1)
            dve.tensor_scalar(wmean[:, 0:k - GH], wmean[:, 0:k - GH], 1.0 / D, None, ALU.mult)
            dve.tensor_scalar(wmean[:, k - GH:k], wmean[:, k - GH:k], 1.0 / GV, None, ALU.mult).then_inc(prep_v, 1)
            dve.wait_ge(prep_v, 2)
            for w, i in wm:
                last = dve.tensor_scalar(w, w, wmean[:, i:i + 1], None, ALU.subtract)
            dve.wait_ge(prep_pe, 1)
            b0, b1_, b2_, b3 = banks[0]
            dve.tensor_copy(gates_w[:], b1_[:, 0:P])
            dve.tensor_copy(csw[:], b2_[:, 0:E]).then_inc(prep_dve, 1)
            dve.tensor_copy(res_w[:, D:D + E], b2_[:, 0:E])
            dve.tensor_copy(res_w[:, 0:D], ident[:])
            dve.tensor_scalar(half_i[:], half_i[:], GK, None, ALU.bitwise_and).then_inc(prep_v, 1)
            dve.wait_ge(prep_v, 3)
            dve.tensor_copy(half_f[:], half_i[:]).then_inc(prep_v, 1)
            dve.wait_ge(prep_v, 4)
            for f in range(2):
                a, b = ((-1.0 / GK, 1.0), (1.0 / GK, 0.0))[f]
                dve.tensor_scalar(half_sel[:, f:f + 1], half_f[:], a, b, ALU.mult, ALU.add)
                dve.tensor_scalar(half_scale[:, f:f + 1], half_f[:], a * GK ** -0.5, b * GK ** -0.5, ALU.mult, ALU.add)
            for l in range(LAYERS):
                for i, name in enumerate(("bq", "bk")):
                    dve.tensor_tensor(zcol[:, 2 * i, l:l + 1], b0[:, 3 * l + i:3 * l + i + 1], col(l, name), ALU.add)
                dve.tensor_tensor(zcol[:, 4, l:l + 1], b0[:, 3 * l + 2:3 * l + 3], col(l, "bv"), ALU.add)
                for j in range(FB):
                    dve.tensor_tensor(zb1[:, l, j:j + 1], b0[:, 32 + FB * l + j:33 + FB * l + j], col(l, f"b1_{j}"),
                                      ALU.add)
            dve.tensor_copy(zmix[:], b0[:, 16:16 + LAYERS])
            dve.tensor_copy(zdown[:], b0[:, 20:20 + LAYERS])
            dve.tensor_copy(zcen[:], b0[:, 24:25]).then_inc(prep_v, 1)
            dve.wait_ge(prep_v, 5)
            for i in range(2):
                dve.tensor_scalar(zcol[:, 2 * i + 1, :], zcol[:, 2 * i, :], 1.0, None, ALU.add)
            for l in range(LAYERS):
                if l:
                    g = col(l - 1, "ln2_g")
                    for w in (wqs, wks, wvs):
                        dve.tensor_scalar(w[:, l, :], w[:, l, :], g, None, ALU.mult)
                    dve.tensor_scalar(res1[:, l, :], centre[:], g, None, ALU.mult)
                else:
                    dve.tensor_copy(res1[:, l, :], centre[:])
                g = col(l, "ln1_g")
                dve.tensor_scalar(w1s[:, l, :], w1s[:, l, :], g, None, ALU.mult)
                dve.tensor_scalar(res2[:, l, :], centre[:], g, None, ALU.mult)
            dve.tensor_scalar(res3[:], centre[:], col(LAYERS - 1, "ln2_g"), None, ALU.mult)
            dve.memset(before[:, 0, :], 0.0)
            dve.wait_ge(prep_pe, 2)
            dve.tensor_copy(out_w[:, D:D + E], b3[:, 0:E]).then_inc(prep_v, 1)
            dve.wait_ge(prep_v, 6)

            dve.memset(id_row[:, B:], 0.0)
            dve.tensor_scalar(id_wrap[:], ids[:], 0.0, float(VOCAB), ALU.is_lt, ALU.mult)
            dve.tensor_copy(id_float[:], ids[:]).then_inc(prep_v, 1)
            dve.wait_ge(prep_v, 7)
            dve.tensor_tensor(id_float[:], id_wrap[:], id_float[:], ALU.add).then_inc(prep_v, 1)
            dve.wait_ge(prep_v, 8)
            dve.tensor_scalar(id_row[:, 0:B], id_float[:], 0.0, float(VOCAB - 1), ALU.max, ALU.min).then_inc(prep_v, 1)
            dve.wait_ge(prep_v, 9)

            def token_rows(it, s):
                dve.tensor_copy(idx[s][:], id_row[:, bass.ds(it * (STREAMS * SEQS) + s * SEQS, SEQS)]) \
                    .then_inc(idx_done[s], 1)

            for s in range(STREAMS):
                token_rows(0, s)
            dve.memset(void_col[:], 0.0).then_inc(ready, 1)

            def embed(it, s):
                dve.wait_ge(embT[s], it + 1)
                dve.scalar_tensor_tensor(out=x[s][:].rearrange("p (q t) -> p q t", q=SEQS),
                                         in0=banks[s][0][:].rearrange("p (q t) -> p q t", q=SEQS), scalar=D ** 0.5,
                                         in1=posT[:].unsqueeze(1).to_broadcast([P, SEQS, S]),
                                         op0=ALU.mult, op1=ALU.add).then_inc(x0[s], 1)

            def qkv(it, s, l):
                n = it * (2 * LAYERS) + 2 * l
                dve.wait_ge(s_exp[s], n + 1)
                dve.tensor_scalar(ek[s][:], ek[s][:], 1.0, None, ALU.min).then_inc(s_min[s], 1)
                dve.wait_ge(s_min[s], n + 1)
                dve.scalar_tensor_tensor(out=kf[s][:], in0=banks[s][1][:], scalar=zcol[:, 3, l:l + 1], in1=ek[s][:],
                                         op0=ALU.add, op1=ALU.max).then_inc(s_elu[s], 1)
                dve.wait_ge(s_exp[s], n + 2)
                dve.tensor_scalar(eq[s][:], eq[s][:], 1.0, -1.0, ALU.min, ALU.add).then_inc(s_min[s], 1)
                dve.wait_ge(s_qkv[s], it * (3 * LAYERS) + 3 * l + 3)
                dve.wait_ge(s_elu[s], n + 1)
                dve.scalar_tensor_tensor(out=kv[s][:], in0=banks[s][2][:], scalar=zcol[:, 4, l:l + 1], in1=kf[s][:],
                                         op0=ALU.add, op1=ALU.mult).then_inc(s_kv[s], 1)
                dve.wait_ge(s_min[s], n + 2)
                dve.scalar_tensor_tensor(out=qf[s][:], in0=banks[s][0][:], scalar=zcol[:, 0, l:l + 1], in1=eq[s][:],
                                         op0=ALU.add, op1=ALU.max).then_inc(s_elu[s], 1)

            def sums(it, s, l):
                dve.wait_ge(s_elu[s], it * (2 * LAYERS) + 2 * l + 2)
                dve.wait_ge(s_sum[s], it * (2 * LAYERS) + 2 * l + 1)
                dve.scalar_tensor_tensor(out=t[s][:], in0=qf[s][:], scalar=1.0, in1=banks[s][3][:],
                                         op0=ALU.add, op1=ALU.mult).then_inc(s_tu[s], 1)
                dve.wait_ge(s_sum[s], it * (2 * LAYERS) + 2 * l + 2)
                dve.scalar_tensor_tensor(out=u[s][:], in0=qf[s][:], scalar=1.0, in1=banks[s][1][:],
                                         op0=ALU.add, op1=ALU.mult).then_inc(s_tu[s], 1)
                dve.wait_ge(s_tu[s], it * (2 * LAYERS) + 2 * l + 2)
                dve.wait_ge(s_rcp[s], it * (2 * LAYERS) + 2 * l + 2)
                dve.tensor_tensor(cx[s][:], u[s][:], t[s][:], ALU.mult).then_inc(s_cx[s], 1)

            def normed(it, s, n, b, shift, dst):
                dve.wait_ge(s_rs[s], it * (2 * PER_Y) + 2 * n + 2)
                dve.scalar_tensor_tensor(out=dst, in0=banks[s][b][:], scalar=shift, in1=rs[s][:],
                                         op0=ALU.add, op1=ALU.mult).then_inc(s_y[s], 1)

            def up(it, s, l):
                for j, b in ((1, 1), (3, 0)):
                    dve.wait_ge(s_h[s], it * (FB * LAYERS) + FB * l + j + 1)
                    dve.tensor_scalar(hid[s][:, j, :], banks[s][b][:], zb1[:, l, j:j + 1], 0.0, ALU.add, ALU.max) \
                        .then_inc(s_relu[1][s], 1)

            def gates(it, s):
                dve.wait_ge(g_proj[s], it * 5 + 1)
                dve.wait_ge(g_act[s], it * NG_ACT + 1)
                dve.tensor_scalar(mn[s][:], banks[s][0][:], gbs[:], 0.0, ALU.add, ALU.min).then_inc(g_dve[s], 1)
                dve.wait_ge(g_proj[s], it * 5 + 4)
                dve.tensor_scalar(hid[s][:, 2, :], banks[s][3][:], -40.0, None, ALU.max).then_inc(g_dve[s], 1)
                dve.wait_ge(g_act[s], it * NG_ACT + 3)
                dve.wait_ge(g_dve[s], it * NG_DVE + 1)
                dve.tensor_tensor(lsp[s][:], mn[s][:], lsp[s][:], ALU.subtract).then_inc(g_dve[s], 1)
                dve.wait_ge(g_dve[s], it * NG_DVE + 3)
                dve.tensor_tensor_scan(G[s][:], restart[:].rearrange("p q t -> p (q t)"), lsp[s][:], 0.0,
                                       ALU.mult, ALU.add).then_inc(g_dve[s], 1)

            def decay(it, s):
                dve.wait_ge(g_dve[s], it * NG_DVE + 4)
                n = it * NG_DVE
                g3 = G[s][:].rearrange("p (q t) -> p q t", q=SEQS)
                mids = [g3[:, :, f * HALF + HALF // 2 - 1] for f in range(2)]
                dve.tensor_scalar(ref_a[s][:], mids[0], half_sel[:, 0:1], None, ALU.mult).then_inc(g_dve[s], 1)
                dve.wait_ge(g_dve[s], n + 5)
                dve.scalar_tensor_tensor(out=ref[s][:], in0=mids[1], scalar=half_sel[:, 1:2], in1=ref_a[s][:],
                                         op0=ALU.mult, op1=ALU.add).then_inc(g_dve[s], 1)
                dve.wait_ge(g_dve[s], n + 6)
                d3 = dG[s][:].rearrange("p (q t) -> p q t", q=SEQS)
                dve.tensor_tensor(d3, g3, ref[s][:].unsqueeze(2).to_broadcast([P, SEQS, S]), ALU.subtract) \
                    .then_inc(g_dve[s], 1)
                dve.wait_ge(g_dve[s], n + 7)
                dve.tensor_scalar(dG[s][:], dG[s][:], -DECAY_MAX, DECAY_MAX, ALU.max, ALU.min).then_inc(g_dve[s], 1)
                dve.wait_ge(g_proj[s], it * 5 + 2)
                dve.wait_ge(g_act[s], it * NG_ACT + 8)
                for f in range(2):
                    a = [x_[:].rearrange("p (q f t) -> p f q t", q=SEQS, f=2)[:, f] for x_ in (Q[s], banks[s][1], eQ[s])]
                    dve.scalar_tensor_tensor(out=a[0], in0=a[1], scalar=half_scale[:, f:f + 1], in1=a[2],
                                             op0=ALU.mult, op1=ALU.mult).then_inc(g_dve[s], 1)
                dve.wait_ge(g_proj[s], it * 5 + 3)
                dve.wait_ge(g_act[s], it * NG_ACT + 9)
                dve.tensor_tensor(K[s][:], banks[s][2][:], eK[s][:], ALU.mult).then_inc(g_dve[s], 1)
                dve.wait_ge(g_act[s], it * NG_ACT + 6)
                dve.wait_ge(g_hT[s], it + 1)
                dve.tensor_tensor(gsil[s][:], banks[s][3][:], hid[s][:, 1, :], ALU.mult).then_inc(g_dve[s], 1)

            def scores(it, s):
                dve.wait_ge(g_score[s], it * GH + 1)
                for h in range(GH):
                    dve.wait_ge(g_score[s], it * GH + h + 1)
                    dve.tensor_tensor(hid[s][:, h, :].rearrange("p (q t) -> p q t", q=SEQS),
                                      banks[s][h][:].rearrange("p (q t) -> p q t", q=SEQS),
                                      causal[:].unsqueeze(1).to_broadcast([P, SEQS, S]), ALU.mult) \
                        .then_inc(g_mask[s], 1)

            def ovar(it, s):
                dve.wait_ge(g_act[s], it * NG_ACT + 12)
                dve.tensor_tensor(u[s][:], banks[s][0][:], rs[s][:], ALU.mult).then_inc(g_dve[s], 1)

            def project(it, s):
                n = it * R_DVE
                dve.wait_ge(r_act[s], it * R_ACT + 1)
                for q in range(SEQS):
                    last = dve.bn_stats(st[s][:, q, :], row[s][:, q, 0:D])
                last.then_inc(r_dve[s], 1)
                wait_alone(dve, r_dve[s], n + 1)
                for q in range(SEQS):
                    last = dve.bn_aggr(mv[s][:, q, :], st[s][:, q, :])
                last.then_inc(r_dve[s], 1)

            def bc(a, n=E):
                return a.unsqueeze(2).to_broadcast([P, SEQS, n])

            def stats(it, s):
                n = it * R_DVE
                dve.wait_ge(r_act[s], it * R_ACT + 3)
                for i in range(2):
                    raw = banks[s][2 + i][:, 0:2 * (D + E)].rearrange("p (q d) -> p q d", q=2)[:, :, D:D + E]
                    last = dve.tensor_tensor(lg[s][:, 2 * i:2 * i + 2, :], raw,
                                             row[s][:, 2 * i:2 * i + 2, D + 1:D + 2].to_broadcast([P, 2, E]), ALU.mult)
                last.then_inc(r_dve[s], 1)
                dve.wait_ge(r_dve[s], n + 3)
                dve.tensor_tensor(lg[s][:], lg[s][:], sbs[:].unsqueeze(1).to_broadcast([P, SEQS, E]), ALU.add) \
                    .then_inc(r_dve[s], 1)
                dve.wait_ge(r_dve[s], n + 4)
                dve.tensor_reduce(mx[s][:], lg[s][:], AX_X, ALU.max).then_inc(r_dve[s], 1)
                dve.wait_ge(r_dve[s], n + 5)
                dve.tensor_tensor(lgm[s][:], lg[s][:], bc(mx[s][:]), ALU.subtract).then_inc(r_dve[s], 1)
                dve.tensor_tensor(cand[s][:], lg[s][:], bc(mx[s][:]), ALU.is_equal).then_inc(r_dve[s], 1)
                dve.wait_ge(r_dve[s], n + 7)
                dve.tensor_tensor(cand[s][:], cand[s][:], rank[:], ALU.mult).then_inc(r_dve[s], 1)
                dve.wait_ge(r_dve[s], n + 8)
                dve.tensor_reduce(m2[s][:], cand[s][:], AX_X, ALU.max).then_inc(r_dve[s], 1)
                dve.wait_ge(r_dve[s], n + 9)
                dve.tensor_tensor(oh[s][:], rank[:], bc(m2[s][:]), ALU.is_equal).then_inc(r_dve[s], 1)
                dve.tensor_tensor(ohb[s][:], rank[:], bc(m2[s][:]), ALU.is_equal).then_inc(r_dve[s], 1)

            def route(it, s):
                n = it * R_DVE
                dve.wait_ge(r_act[s], it * R_ACT + 4)
                dve.tensor_reduce(sm[s][:], ex[s][:], AX_X, ALU.add).then_inc(r_dve[s], 1)
                dve.wait_ge(r_dve[s], n + 12)
                dve.reciprocal(row[s][:, :, D + 2], sm[s][:]).then_inc(r_dve[s], 1)
                dve.wait_ge(r_dve[s], n + 13)
                dve.tensor_tensor(sc1[s][:], row[s][:, :, D + 1], row[s][:, :, D + 2], ALU.mult).then_inc(r_dve[s], 1)
                dve.tensor_copy(row[s][:, :, D], mv[s][:, :, 0]).then_inc(r_dve[s], 1)
                dve.wait_ge(r_dve[s], n + 14)
                dve.tensor_scalar(sc2[s][:], sc1[s][:], 1.0, None, ALU.add).then_inc(r_dve[s], 1)
                dve.scalar_tensor_tensor(out=sc3[s][:], in0=sc1[s][:], scalar=-1.0, in1=mv[s][:, :, 0],
                                         op0=ALU.mult, op1=ALU.mult).then_inc(r_dve[s], 1)
                dve.tensor_scalar(row[s][:, :, D + 3], token_no[:], tile_start[s][:], None, ALU.add) \
                    .then_inc(r_dve[s], 1)
                dve.wait_ge(r_dve[s], n + 18)
                dve.tensor_scalar(tile_start[s][:], tile_start[s][:], float(STREAMS * TILE), None, ALU.add) \
                    .then_inc(r_dve[s], 1)
                dve.wait_ge(r_cnt[s], it + 1)
                o = s * SEQS
                for q in range(SEQS):
                    dve.tensor_tensor(before[:, o + q + 1, :], before[:, o + q, :],
                                      banks[s][1][:, (SEQS + q) * E:(SEQS + q + 1) * E], ALU.add) \
                        .then_inc(r_before, 1)
                    dve.wait_ge(r_before, it * (R_BEF) + o + q + 1)

            def slots(it, s):
                m = it * 7
                cnt = banks[s][1][:, 0:SEQS * E].rearrange("p (q e) -> p q e", q=SEQS)
                dve.tensor_tensor(pick[s][:], cnt, before[:, s * SEQS:(s + 1) * SEQS, :], ALU.add) \
                    .then_inc(r_slot[s], 1)
                dve.wait_ge(r_slot[s], m + 1)
                dve.tensor_tensor(pick[s][:], pick[s][:], oh[s][:], ALU.mult).then_inc(r_slot[s], 1)
                if s == STREAMS - 1:
                    dve.tensor_copy(before[:, 0, :], before[:, STREAMS * SEQS, :]).then_inc(r_before, 1)
                    dve.wait_ge(r_before, it * R_BEF + R_BEF)
                dve.wait_ge(r_slot[s], m + 2)
                dve.tensor_reduce(place[s][:], pick[s][:], AX_X, ALU.add).then_inc(r_slot[s], 1)
                dve.tensor_scalar(slot_f[s][:], m2[s][:], -float(SLOTS), float(E * SLOTS - 1), ALU.mult, ALU.add) \
                    .then_inc(r_slot[s], 1)
                dve.wait_ge(r_slot[s], m + 4)
                dve.tensor_scalar(over[s][:], place[s][:], float(CAP), FAR, ALU.is_gt, ALU.mult).then_inc(r_slot[s], 1)
                dve.tensor_tensor(slot_f[s][:], slot_f[s][:], place[s][:], ALU.add).then_inc(r_slot[s], 1)
                dve.wait_ge(r_slot[s], m + 6)
                dve.tensor_tensor(slot[s][:], slot_f[s][:], over[s][:], ALU.add).then_inc(r_slot[s], 1)

            def stage(it, s, name):
                if name == "embed":
                    embed(it, s)
                    dve.wait_ge(rows_in[s], it * (16 * SEQS) + 16 * SEQS)
                    token_rows(it + 1, s)
                elif name == "cvar":
                    normed(it, s, 2 * LAYERS, 0, zcen[:], hid[s][:, 0, :])
                elif name == "gates":
                    gates(it, s)
                elif name == "decay":
                    decay(it, s)
                elif name == "scores":
                    scores(it, s)
                elif name == "ovar":
                    ovar(it, s)
                elif name == "project":
                    project(it, s)
                elif name == "stats":
                    stats(it, s)
                elif name == "route":
                    route(it, s)
                elif name == "slots":
                    slots(it, s)
                elif name[0] == "qkv":
                    qkv(it, s, name[1])
                elif name[0] == "sums":
                    sums(it, s, name[1])
                elif name[0] == "var1":
                    normed(it, s, 2 * name[1], 0, zmix[:, name[1]:name[1] + 1], n1[s][:])
                elif name[0] == "up":
                    up(it, s, name[1])
                elif name[0] == "var2":
                    normed(it, s, 2 * name[1] + 1, 3, zdown[:, name[1]:name[1] + 1], x[s][:])

            for at in stage_order(0):
                stage(*at)
            with dve.Fori(0, PAIRS - 1) as j:
                for at in stage_order(j + 1, before=j):
                    stage(*at)
            for at in last_stages(PAIRS - 1):
                stage(*at)

            def row_number(e, b):
                dve.tensor_copy(idp[b][:], xin[b][:, :, D + 3]).then_inc(f_id, 1)

            def norm_chunk(e2, i):
                b, c = i // CHUNKS, i % CHUNKS
                if c == 0:
                    dve.wait_ge(f_in[b], e2 * 16 + 16)
                    dve.wait_ge(f_free[b], e2 + 1)
                    row_number(e2, b)
                if i >= 4:
                    dve.wait_ge(f_tr, e2 * (2 * CHUNKS) + i - 3)
                dve.tensor_scalar(xfn[i % 4][:, 0:D], xin[b][:, c, 0:D], xin[b][:, c, D:D + 1],
                                  xin[b][:, c, D + 1:D + 2], ALU.subtract, ALU.mult).then_inc(f_xf, 1)

            def finish_chunk(e2, i):
                b, c = i // CHUNKS, i % CHUNKS
                dve.wait_ge(f_y, e2 * (2 * CHUNKS) + i + 1)
                dve.scalar_tensor_tensor(out=yo[b][:, c, :], in0=fyb[i % 4][:, 0:D], scalar=xin[b][:, c, D + 2:D + 3],
                                         in1=xin[b][:, c, 0:D], op0=ALU.mult, op1=ALU.add).then_inc(f_o, 1)

            with dve.Fori(0, E // 2) as e2:
                for i in range(2 * CHUNKS + 3):
                    if i < 2 * CHUNKS:
                        norm_chunk(e2, i)
                    if i >= 3:
                        finish_chunk(e2, i - 3)


        @block.gpsimd
        def _(pool):
            pool.memset(void_row[:], FAR)
            pool.memset(onesf[:], 1.0).then_inc(const2, 1)
            for a, v in ((ident, 0.0), (mean_all, 1.0 / D), (ones_b, 1.0), (ones_r, 1.0),
                         (eps_attn, 1e-6), (eps_tower, 1e-3), (eps_norm, 1e-5), (one_c, 1.0), (restart, 1.0),
                         (tile_start[0], 0.0), (tile_start[1], float(TILE))):
                last = pool.memset(a[:], v)
            last.then_inc(pool_step, 1)
            pool.wait_ge(pool_step, 1)
            pool.memset(restart[:, :, 0:1], 0.0)
            pool.affine_select(out=ident[:], in_=ident[:], compare_op=ALU.not_equal, fill=1.0, base=0,
                               pattern=[[-1, P]], channel_multiplier=1).then_inc(pool_step, 1)
            pool.affine_select(out=causal[:], in_=onesf[:], compare_op=ALU.is_ge, fill=0.0, base=0,
                               pattern=[[1, P]], channel_multiplier=-1).then_inc(pool_step, 1)
            for m, w in ((head_sum, HEAD), (mean_v, GV)):
                pool.affine_select(out=m[:].rearrange("p (g c) -> p g c", c=w),
                                   in_=onesf[:].rearrange("p (g c) -> p g c", c=w), compare_op=ALU.is_ge, fill=0.0,
                                   base=0, pattern=[[-w, P // w], [0, w]], channel_multiplier=1).then_inc(pool_step, 1)
            pool.wait_ge(pool_step, 5)
            for m, w in ((head_sum, HEAD), (mean_v, GV)):
                pool.affine_select(out=m[:].rearrange("p (g c) -> p g c", c=w),
                                   in_=m[:].rearrange("p (g c) -> p g c", c=w), compare_op=ALU.is_ge, fill=0.0,
                                   base=w - 1, pattern=[[w, P // w], [0, w]], channel_multiplier=-1) \
                    .then_inc(pool_step, 1)
            pool.tensor_copy(tri[:], causal[:]).then_inc(const, 1)
            pool.iota(rank_i[:], [[0, SEQS], [-1, E]], base=E, channel_multiplier=0).then_inc(pool_step, 1)
            pool.iota(token_i[:], [[S, SEQS]], base=0, channel_multiplier=1).then_inc(pool_step, 1)
            pool.iota(half_i[:], [[0, 1]], base=0, channel_multiplier=1).then_inc(pool_step, 1)
            pool.wait_ge(pool_step, 10)
            pool.tensor_scalar(mean_v[:], mean_v[:], 1.0 / GV, None, ALU.mult).then_inc(const, 1)
            pool.tensor_copy(rank[:], rank_i[:])
            pool.tensor_copy(token_no[:], token_i[:]).then_inc(const, 1)
            pool.tensor_tensor(centre[:], ident[:], mean_all[:], ALU.subtract).then_inc(const, 1)

            def gather(it, s):
                wait_alone(pool, idx_done[s], it + 1)
                for q in range(SEQS):
                    pool.indirect_dma_start(rows[s][:, q, :], None, emb, bass.IndirectOffsetOnAxis(
                        ap=idx[s][:, q:q + 1], axis=0), bounds_check=VOCAB - 1, oob_is_err=False) \
                        .then_inc(rows_in[s], 16)

            for s in range(STREAMS):
                gather(0, s)
                pool.sem_inc(row_free[s], 1)
                pool.sem_inc(plain_free[s], 1)
            for b in range(2):
                pool.sem_inc(f_free[b], 1)
            pool.sem_inc(f_o, 4)
            pool.wait_ge(void_out, 16 * E)
            pool.wait_ge(ready, 1)

            def centre_(it, s):
                i = (LAYERS - 1) * NV
                g, b = i + VEC.index("ln2_g"), i + VEC.index("ln2_b")
                wait_alone(pool, s_y[s], it * PER_Y + 2 * LAYERS)
                pool.tensor_scalar(hT[s][:], x[s][:], vecs[:, g:g + 1], vecs[:, b:b + 1], ALU.mult, ALU.add) \
                    .then_inc(g_hT[s], 1)

            def ovar(it, s):
                pool.wait_ge(g_dve[s], it * NG_DVE + 13)
                pool.tensor_tensor(cx[s][:], u[s][:], gsil[s][:], ALU.mult).then_inc(g_pool[s], 1)

            def scatter(it, s):
                pool.wait_ge(r_slot[s], it * 7 + 7)
                wait_alone(pool, r_dve[s], it * R_DVE + 19)
                for q in range(SEQS):
                    pool.indirect_dma_start(slots_dram, bass.IndirectOffsetOnAxis(ap=slot[s][:, q:q + 1], axis=0),
                                            row[s][:, q, :], None, bounds_check=E * SLOTS - 1, oob_is_err=False) \
                        .then_inc(row_out[s], 16)

            def stage(it, s, name):
                if name == ("up", 0):
                    pool.wait_ge(embT[s], it + 1)
                    gather(it + 1, s)
                elif name == "centre":
                    centre_(it, s)
                elif name == "ovar":
                    ovar(it, s)
                elif name == "slots":
                    scatter(it, s)

            for at in stage_order(0):
                stage(*at)
            with pool.Fori(0, PAIRS - 1) as j:
                for at in stage_order(j + 1, before=j):
                    stage(*at)
            for at in last_stages(PAIRS - 1):
                stage(*at)
            for s in range(STREAMS):
                pool.wait_ge(rows_in[s], 16 * SEQS * (PAIRS + 1))
                pool.wait_ge(plain_out[s], 16 * PAIRS)

            with pool.Fori(0, E // 2) as e2:
                for b in range(2):
                    for c in range(CHUNKS):
                        wait_alone(pool, f_o, e2 * (2 * CHUNKS) + b * CHUNKS + c + 5)
                        pool.indirect_dma_start(out, bass.IndirectOffsetOnAxis(ap=idp[b][:, c:c + 1], axis=0),
                                                yo[b][:, c, :], None, bounds_check=N - 1, oob_is_err=False) \
                            .then_inc(f_out[b], 16)



_VECS = {"bq": "L0_tok_bq", "bk": "L0_tok_bk", "bv": "L0_tok_bv", "bo": "L0_tok_bo", "ln1_g": "L0_tok_ln1_g",
         "ln1_b": "L0_tok_ln1_b", "b2": "L0_tok_b2", "ln2_g": "L0_tok_ln2_g", "ln2_b": "L0_tok_ln2_b"}


def kernel(**inputs):
    import numpy as np
    import concourse.bacc as bacc
    from concourse.bass_utils import run_bass_kernel_spmd as run

    a = {k: np.asarray(v) for k, v in inputs.items()}
    columns = []
    for l in range(LAYERS):
        for name in VEC:
            if name in _VECS:
                columns.append(a[_VECS[name]][l])
            else:
                j = int(name[-1])
                columns.append(a["L0_tok_b1"][l, j * P:(j + 1) * P])
    ins = [
        ("tok", a["x"].T),
        ("emb", a["L0_tok_emb"]),
        ("pos", a["L0_tok_pos_enc"][:S].T),
        ("wq", a["L0_tok_Wq"]), ("wk", a["L0_tok_Wk"]), ("wv", a["L0_tok_Wv"]), ("wo", a["L0_tok_Wo"]),
        ("w1", a["L0_tok_W1"]), ("w2", a["L0_tok_W2"]),
        ("vec", np.stack(columns, axis=1)),
        ("gq", a["L0_attn_Wq"]), ("gk", a["L0_attn_Wk"]), ("gv", a["L0_attn_Wv"]), ("gg", a["L0_attn_Wg"]),
        ("gk1_t", a["L0_attn_Wgk1"].T), ("gk2", a["L0_attn_Wgk2"]), ("gb", a["L0_attn_bgk2"].reshape(-1, 1)),
        ("go", a["L0_attn_Wo"]), ("go_t", a["L0_attn_Wo"].T),
        ("sw", a["L0_ffn_switch_w"].T), ("sb", a["L0_ffn_switch_b"]),
        ("ew", a["L0_ffn_expert_w"].transpose(2, 0, 1)), ("eb", a["L0_ffn_expert_b"].reshape(1, E, D)),
    ]
    nc = bacc.Bacc("TRN2", target_bir_lowering=False, num_devices=1)
    arrays, args = {}, []
    for name, v in ins:
        v = np.ascontiguousarray(v)
        arrays[f"in_{name}"] = v
        args.append(nc.dram_tensor(f"in_{name}", v.shape, mybir.dt.from_np(v.dtype), kind="ExternalInput").ap())
    b = a["x"].shape[0]
    args.append(nc.dram_tensor("out_rows", (b * S, D), F32, kind="ExternalOutput").ap())
    build(nc, *args)
    r = run(nc, [arrays], core_ids=[0])
    return r.results[0]["out_rows"].reshape(b, S, D)
```

```python
from contextlib import ExitStack

import concourse.bass as bass
from concourse import mybir

F32 = mybir.dt.float32
F32R = mybir.dt.float32r
BF16 = mybir.dt.bfloat16
I32 = mybir.dt.int32
U32 = mybir.dt.uint32
ALU = mybir.AluOpType
ACT = mybir.ActivationFunctionType
AX_X = mybir.AxisListType.X

P = 128
D = 128
LAYERS = 4
HEAD = 16
DFF = 512
FB = DFF // P
S = 128
SEQS = 4
TILE = SEQS * S
STREAMS = 2
GH = 4
GK = 16
GV = 32
HALF = S // 2
E = 16
ROW = D + 4
CHUNKS = 10
SLOTS = CHUNKS * P
FAR = 1.0e6
DECAY_MAX = 960.0

VEC = ["bq", "bk", "bv", "bo", "ln1_g", "ln1_b", "b2", "ln2_g", "ln2_b", "b1_0", "b1_1", "b1_2", "b1_3"]
NV = len(VEC)

STAGES = ["embed"]
for _l in range(LAYERS):
    STAGES += [(n, _l) for n in ("qkv", "sums", "mix", "var1", "up", "down", "var2")]
STAGES += ["centre", "cvar", "gates", "values", "decay", "scores", "outs", "ovar", "project", "stats", "route", "slots"]


TURNS = {
    "pe": (
        "acaaacacaaaccacaccaaaaaaaaacaccccaccacaacaaacaacbaaaaaaabbbabababbbaaabaaaabbbbbababbbaabaaaabbb"
        "abababbabbaaaabbbbabaabababbbaaaaaaabbaabbabbababbaaaabbbbabbbbbbaaaabbbababaababbbabbbbbbbbab"),
    "act": (
        "acacccaaaccaaccccaacaccaaaaacaccaacaccaacaacacaccbbabababaabbaabbabbaababbababababababbaabaabbab"
        "aabbabaaababaaababaabbbaaabababbaaaabbbbbbabaabbbababababbaaabba"),
    "dve": (
        "aaaacaaaaaacaaccaaaccccccccccccaacacaaaaaccaaacccccccccccaacacccccccccccccccbbbbbbbbbbbbaaaaaaab"
        "ababaaaaabbbbbbbbbbbaaabbbaaaaaaaaaaabbbbbbbbabbbabbbaaaaaaaaaaaabbbaaabbbbabbbbaabbbaaaaaaaaaaa"
        "aaaaaaaaaaaaaaaa"),
    "pool": (
        "aaccaccaba"),
}
CUT = {"pe": ("var2", 3), "act": "centre", "dve": ("var2", 3), "pool": "slots"}


def steps(stage, it, s, first=0, last=len(STAGES)):
    for name in STAGES[first:last]:
        yield from stage(it, s, name)


def take_turns(engine, stage, it, before):
    cut = STAGES.index(CUT[engine])
    runs = {}
    if it is not None:
        runs["a"] = steps(stage, it, 0)
        runs["b"] = steps(stage, it, 1, 0, cut)
    if before is not None:
        runs["c"] = steps(stage, before, 1, cut)
    for turn in TURNS[engine]:
        if turn in runs:
            next(runs[turn])
    for run in runs.values():
        assert next(run, "end") == "end"


def build(nc, tok, emb, pos, wq, wk, wv, wo, w1, w2, vec, gq, gk, gv, gg, gk1_t, gk2, gb, go, go_t, sw, sb, ew, eb, out):
    VOCAB = emb.shape[0]
    B = tok.shape[1]
    N = B * S
    TILES = B // SEQS
    PAIRS = TILES // STREAMS
    CAP = int(1.2 * N / E)
    assert CAP <= SLOTS and E * SLOTS < FAR and N < FAR

    with ExitStack() as ctx:
        def sbuf(name, shape, dt=F32):
            return ctx.enter_context(nc.sbuf_tensor(name, shape, dt))

        def sem(name):
            return ctx.enter_context(nc.semaphore(name))

        slots_dram = nc.dram_tensor("slot_rows", (E * SLOTS, ROW), F32, kind="Internal").ap()

        ident = sbuf("ident", [P, P])
        centre = sbuf("centre", [P, P])
        mean_all = sbuf("mean_all", [P, P])
        head_sum = sbuf("head_sum", [P, P])
        mean_v = sbuf("mean_v", [P, P])
        causal = sbuf("causal", [P, P])
        tri = sbuf("tri", [P, P], BF16)
        ones_b = sbuf("ones_b", [P, P], BF16)
        ones_r = sbuf("ones_r", [1, P])
        onesf = sbuf("onesf", [P, P])
        restart = sbuf("restart", [P, SEQS, S])
        eps_attn = sbuf("eps_attn", [P, 1])
        eps_tower = sbuf("eps_tower", [P, 1])
        eps_norm = sbuf("eps_norm", [P, 1])
        one_c = sbuf("one_c", [P, 1])
        half_i = sbuf("half_i", [P, 1], I32)
        half_f = sbuf("half_f", [P, 1])
        half_sel = sbuf("half_sel", [P, 2])
        half_scale = sbuf("half_scale", [P, 2])
        rank = sbuf("rank", [P, SEQS, E])
        token_no = sbuf("token_no", [P, SEQS])
        void_row = sbuf("void_row", [P, ROW])

        vecs = sbuf("vecs", [P, LAYERS * NV])
        zcol = sbuf("zcol", [P, 5, LAYERS])
        zb1 = sbuf("zb1", [P, LAYERS, FB])
        zmix = sbuf("zmix", [P, LAYERS])
        zdown = sbuf("zdown", [P, LAYERS])
        zcen = sbuf("zcen", [P, 1])
        work = sbuf("work", [P, LAYERS, 2])
        wqs = sbuf("wqs", [P, LAYERS, D])
        wks = sbuf("wks", [P, LAYERS, D])
        wvs = sbuf("wvs", [P, LAYERS, D])
        wos = sbuf("wos", [P, LAYERS, D])
        w1s = sbuf("w1s", [P, LAYERS, DFF])
        w2s = sbuf("w2s", [P, LAYERS, FB, D])
        wmean = sbuf("wmean", [P, LAYERS * (FB + 1) + GH])
        res1 = sbuf("res1", [P, LAYERS, D])
        res2 = sbuf("res2", [P, LAYERS, D])
        split_w = {n: [sbuf(f"{n}_{part}", [P, LAYERS, w], F32R) for part in ("hi", "lo")]
                   for n, w in (("q", D), ("k", D), ("v", D), ("up", DFF), ("res1", D), ("res2", D))}
        res3 = sbuf("res3", [P, D])
        gqs = sbuf("gqs", [P, P])
        gks = sbuf("gks", [P, P])
        gvs = sbuf("gvs", [P, D])
        ggs = sbuf("ggs", [P, D])
        gk1s = sbuf("gk1s", [GK, P])
        gk2s = sbuf("gk2s", [GK, P])
        gates_w = sbuf("gates_w", [P, P])
        gbs = sbuf("gbs", [P, 1])
        goT = sbuf("goT", [P, D])
        sws = sbuf("sws", [P, E])
        csw = sbuf("csw", [P, E])
        out_w = sbuf("out_w", [P, D + E])
        res_w = sbuf("res_w", [P, D + E])
        sbs = sbuf("sbs", [P, E])
        ews = sbuf("ews", [P, E, D])
        ebs = sbuf("ebs", [1, E, D])
        posT = sbuf("posT", [P, S])

        def per_stream(name, shape, dt=F32):
            return [sbuf(f"{name}{s}", shape, dt) for s in range(STREAMS)]

        ids = sbuf("ids", [P, B], I32)
        id_wrap = sbuf("id_wrap", [P, B])
        id_float = sbuf("id_float", [P, B])
        id_row = sbuf("id_row", [P, B + STREAMS * SEQS], U32)
        idx = per_stream("idx", [P, SEQS], U32)
        rows = per_stream("rows", [P, SEQS, D])
        x = per_stream("x", [P, TILE])
        x_hi = per_stream("x_hi", [P, TILE], F32R)
        x_lo = per_stream("x_lo", [P, TILE], F32R)
        n1_hi = per_stream("n1_hi", [P, TILE], F32R)
        n1_lo = per_stream("n1_lo", [P, TILE], F32R)
        eq = per_stream("eq", [P, TILE])
        ek = per_stream("ek", [P, TILE])
        qf = per_stream("qf", [P, TILE])
        kf = per_stream("kf", [P, TILE])
        kv = per_stream("kv", [P, TILE])
        t = per_stream("t", [P, TILE])
        u = per_stream("u", [P, TILE])
        cx = per_stream("cx", [P, TILE])
        sq = per_stream("sq", [P, TILE])
        rs = per_stream("rs", [P, TILE])
        n1 = per_stream("n1", [P, TILE])
        hid = per_stream("hid", [P, FB, TILE])
        hT = per_stream("hT", [P, TILE])
        row = per_stream("row", [P, SEQS, ROW])
        plain = per_stream("plain", [P, SEQS, D])
        st = per_stream("st", [P, SEQS, 6])
        mv = per_stream("mv", [P, SEQS, 2])
        lnv = per_stream("lnv", [P, SEQS])
        sc1 = per_stream("sc1", [P, SEQS])
        sc2 = per_stream("sc2", [P, SEQS])
        sc3 = per_stream("sc3", [P, SEQS])
        ref = per_stream("ref", [P, SEQS])
        ref_a = per_stream("ref_a", [P, SEQS])
        lg = per_stream("lg", [P, SEQS, E])
        lgm = per_stream("lgm", [P, SEQS, E])
        ex = per_stream("ex", [P, SEQS, E])
        cand = per_stream("cand", [P, SEQS, E])
        oh = per_stream("oh", [P, SEQS, E])
        ohb = per_stream("ohb", [P, SEQS, E], BF16)
        mx = per_stream("mx", [P, SEQS])
        m2 = per_stream("m2", [P, SEQS])
        sm = per_stream("sm", [P, SEQS])
        place = per_stream("place", [P, SEQS])
        over = per_stream("over", [P, SEQS])
        pick = per_stream("pick", [P, SEQS, E])
        slot_f = per_stream("slot_f", [P, SEQS])
        slot = per_stream("slot", [P, SEQS], U32)
        before = sbuf("before", [P, STREAMS * SEQS + 1, E])

        banks = [[ctx.enter_context(nc.psum_tensor(f"bank{s}{i}", [P, 512], F32)) for i in range(4)]
                 for s in range(STREAMS)]

        mn, lsp, G, dG, eQ, eK = eq, ek, t, u, qf, kf
        Q, K, V, gsil = cx, sq, eq, x

        load_ids = sem("load_ids")
        load_w = sem("load_w")
        load_e = sem("load_e")
        prep_ids = sem("prep_ids")
        prep_mean = sem("prep_mean")
        prep_gain = sem("prep_gain")
        prep_act = sem("prep_act")
        const = sem("const")
        const2 = sem("const2")
        prep_pe = sem("prep_pe")
        prep_dve = sem("prep_dve")
        ready = sem("ready")
        void_out = sem("void_out")

        def each(name):
            return [sem(f"{name}{s}") for s in range(STREAMS)]

        idx_done = each("idx_done")
        rows_in = each("rows_in")
        embT = each("embT")
        x0 = each("x0")
        s_qkv = each("s_qkv")
        s_exp = each("s_exp")
        s_min = each("s_min")
        s_elu = each("s_elu")
        s_kv = each("s_kv")
        s_sum = each("s_sum")
        s_tu = each("s_tu")
        s_rcp = each("s_rcp")
        s_cx = each("s_cx")
        s_z = each("s_z")
        s_sq = each("s_sq")
        s_var = each("s_var")
        s_rs = each("s_rs")
        s_y = each("s_y")
        s_hi = each("s_hi")
        s_lo = each("s_lo")
        s_h = each("s_h")
        s_relu = each("s_relu")
        g_hT = each("g_hT")
        g_proj = each("g_proj")
        g_act = each("g_act")
        g_dve = each("g_dve")
        g_gated = each("g_gated")
        g_score = each("g_score")
        g_mask = each("g_mask")
        g_o = each("g_o")
        g_h2 = each("g_h2")
        r_act = each("r_act")
        r_dve = each("r_dve")
        r_cnt = each("r_cnt")
        row_out = each("row_out")
        plain_out = each("plain_out")

        f_in = [sem("f_in0"), sem("f_in1")]
        f_xf = sem("f_xf")
        f_tr = sem("f_tr")
        f_xT = sem("f_xT")
        f_y = sem("f_y")
        f_o = sem("f_o")
        f_id = sem("f_id")
        f_out = [sem("f_out0"), sem("f_out1")]

        pool_step = sem("pool_step")
        rank_i = sbuf("rank_i", [P, SEQS, E], I32)
        token_i = sbuf("token_i", [P, SEQS], I32)
        prep_v = sem("prep_v")
        row_free = each("row_free")
        plain_free = each("plain_free")
        f_free = [sem("f_free0"), sem("f_free1")]
        r_before = sem("r_before")
        r_slot = each("r_slot")
        tile_start = [sbuf(f"tile_start{s}", [P, 1]) for s in range(STREAMS)]
        R_BEF = STREAMS * SEQS + 1
        ftr = banks[0]
        fyb = banks[1]
        xfT = [t[0], u[0], cx[0], sq[0]]
        zero_col = sbuf("zero_col", [P, 1])
        xin = [w1s[:].rearrange("p l f -> p (l f)")[:, 0:CHUNKS * ROW].rearrange("p (c r) -> p c r", r=ROW),
               sbuf("xin1", [P, CHUNKS, ROW])[:]]
        xfn = [eq[0], ek[0], qf[0], kf[0]]
        idp = [sbuf("idp0", [P, CHUNKS], U32), sbuf("idp1", [P, CHUNKS], U32)]
        yo = [hid[b][:].rearrange("p j (a d) -> p (j a) d", d=D)[:, 0:CHUNKS, :] for b in range(2)]
        NG_ACT = 12
        NG_DVE = 13
        R_ACT = 8
        R_DVE = 19

        WLOADS = 29
        block = ctx.enter_context(nc.Block())

        PER_Y = 2 * LAYERS + 1

        def slot_rows(e):
            return slots_dram[bass.ds(e * SLOTS, SLOTS), :].rearrange("(p c) r -> p c r", p=P)

        alone = {e: sem(f"alone_{e}") for e in ("pool", "dve")}

        def wait_alone(eng, s, value):
            eng.wait_ge(s, value)
            eng.sem_inc(alone["pool" if eng.engine == nc.gpsimd.engine else "dve"], 1)

        @block.sync
        def _(sp):
            loads = [
                (vecs[:], vec), (posT[:], pos), (wqs[:], wq.rearrange("l i o -> i l o")),
                (wks[:], wk.rearrange("l i o -> i l o")), (wvs[:], wv.rearrange("l i o -> i l o")),
                (wos[:], wo.rearrange("l i o -> i l o")), (w1s[:], w1.rearrange("l i o -> i l o")),
                (w2s[:], w2.rearrange("l (j i) o -> i l j o", i=P)),
                (gvs[:], gv), (ggs[:], gg), (gk1s[:], gk1_t), (out_w[:, 0:D], go), (sws[:], sw),
                (sbs[:], sb.partition_broadcast(P)), (goT[:], go_t),
            ]
            with nc.allow_non_contiguous_dma("small operands, once"):
                pads = [(gqs, gq), (gks, gk), (gk2s, gk2)]
                sp.dma_start(ids[:], tok).then_inc(load_ids, 16)
                for dst, src in loads:
                    sp.dma_start(dst, src).then_inc(load_w, 16)
                for f in range(2):
                    for dst, src in pads:
                        sp.dma_start(dst[:].rearrange("p (h f c) -> p f h c", h=GH, f=2)[:, f],
                                     src.rearrange("p (h c) -> p h c", h=GH)).then_inc(load_w, 16)
                    for h in range(GH):
                        sp.dma_start(gbs[32 * h + GK * f:32 * h + GK * (f + 1), :],
                                     gb[h * GK:(h + 1) * GK, :]).then_inc(load_w, 16)
                sp.wait_ge(const2, 1)
                for c in range(E * CHUNKS // 10):
                    sp.dma_start(slots_dram[c * SLOTS:(c + 1) * SLOTS, :].rearrange("(p c) r -> p c r", p=P),
                                 void_row[:].unsqueeze(1).to_broadcast([P, CHUNKS, ROW])).then_inc(void_out, 16)
                for dst, src in ((ews[:], ew), (ebs[:], eb)):
                    sp.dma_start(dst, src).then_inc(load_e, 16)

            def store_plain(it, s):
                sp.wait_ge(r_act[s], it * R_ACT + R_ACT)
                sp.dma_start(out_tile(it, s), plain[s][:]).then_inc(plain_out[s], 16)

            def out_tile(it, s):
                return out[bass.ds(it * (STREAMS * TILE) + s * TILE, TILE), :].rearrange("(q p) d -> p q d", p=P)

            with sp.Fori(0, PAIRS) as it:
                for s in range(STREAMS):
                    store_plain(it, s)
                for s in range(STREAMS):
                    sp.wait_ge(row_out[s], it * (16 * SEQS) + 16 * SEQS)
                    sp.sem_inc(row_free[s], 1)
                    sp.wait_ge(plain_out[s], it * 16 + 16)
                    sp.sem_inc(plain_free[s], 1)
            for s in range(STREAMS):
                sp.wait_ge(plain_out[s], 16 * PAIRS)
            for s in range(STREAMS):
                sp.wait_ge(row_out[s], 16 * SEQS * PAIRS)
            for b in range(2):
                sp.dma_start(xin[b][:], slot_rows(b)).then_inc(f_in[b], 16)
            with sp.Fori(0, E // 2 - 1) as e2:
                for b in range(2):
                    sp.wait_ge(f_o, e2 * (2 * CHUNKS) + (b + 1) * CHUNKS + 4)
                    sp.wait_ge(f_id, e2 * 2 + b + 1)
                    sp.dma_start(xin[b][:], slot_rows(e2 * 2 + b + 2)).then_inc(f_in[b], 16)
                    sp.wait_ge(f_out[b], e2 * (16 * CHUNKS) + 16 * CHUNKS)
                    sp.sem_inc(f_free[b], 1)
            for b in range(2):
                sp.wait_ge(f_out[b], 16 * CHUNKS * E // 2)


        @block.tensor
        def _(pe):
            pe.wait_ge(load_w, 16 * WLOADS)
            pe.wait_ge(const, 5)
            pe.wait_ge(prep_dve, 1)
            b0, b1_, b2_, b3 = banks[0]
            pe.matmul(b1_[:, 0:P], gk1s[:], gk2s[:], start=True, stop=True)
            pe.matmul(b2_[:, 0:E], centre[:], sws[:], start=True, stop=True)
            pe.matmul(b0[:, 0:1], centre[:],
                      vecs[:, (LAYERS - 1) * NV + VEC.index("ln2_b"):(LAYERS - 1) * NV + VEC.index("ln2_b") + 1],
                      start=True, stop=True).then_inc(prep_pe, 1)
            for l in range(LAYERS):
                v = vecs[:, l * NV:(l + 1) * NV]
                if l > 0:
                    beta = vecs[:, (l - 1) * NV + VEC.index("ln2_b"):(l - 1) * NV + VEC.index("ln2_b") + 1]
                else:
                    beta = zero_col[:]
                b = banks[1][l]
                for i, w in enumerate((wqs, wks, wvs)):
                    pe.matmul(b[:, i:i + 1], w[:, l, :], beta, start=True, stop=True)
                g = VEC.index("ln1_b")
                for j in range(FB):
                    pe.matmul(b[:, 5 + j:6 + j], w1s[:, l, j * P:(j + 1) * P], v[:, g:g + 1], start=True, stop=True)
                pe.matmul(b[:, 3:4], centre[:], work[:, l, 0:1], start=True, stop=True)
                pe.matmul(b[:, 4:5], centre[:], work[:, l, 1:2], start=True, stop=True).then_inc(prep_pe, 1)
            pe.wait_ge(prep_dve, 2)
            pe.matmul(b3[:, 0:E], goT[:], csw[:], start=True, stop=True).then_inc(prep_pe, 1)
            pe.wait_ge(ready, 1)

            def embed(it, s):
                b = banks[s][0]
                pe.wait_ge(rows_in[s], it * (16 * SEQS) + 16 * SEQS)
                for q in range(SEQS):
                    mm = pe.transpose(b[:, q * S:(q + 1) * S], rows[s][:, q, :], ident[:])
                mm.then_inc(embT[s], 1)
                yield

            def part(out_, w, l, k, moving, start=False, stop=False, c=slice(None)):
                return pe.matmul(out_[:], split_w[w][k][:, l, c], moving[:], start=start, stop=stop)

            def product(out_, w, l, hi, lo, start, stop, c=slice(None)):
                part(out_, w, l, 0, hi, start=start, c=c)
                part(out_, w, l, 1, hi, c=c)
                return part(out_, w, l, 0, lo, stop=stop, c=c)

            def qkv(it, s, l):
                n = it * (2 * LAYERS) + 2 * l + 1
                bank = {"k": banks[s][1], "q": banks[s][0], "v": banks[s][2]}
                pe.wait_ge(s_hi[s], n)
                part(bank["k"], "k", l, 0, x_hi[s], start=True)
                part(bank["k"], "k", l, 1, x_hi[s])
                if l > 0:
                    part(bank["q"], "q", l, 0, x_hi[s], start=True)
                yield
                pe.wait_ge(s_lo[s], n)
                part(bank["k"], "k", l, 0, x_lo[s], stop=True).then_inc(s_qkv[s], 1)
                yield
                if l == 0:
                    part(bank["q"], "q", l, 0, x_hi[s], start=True)
                part(bank["q"], "q", l, 1, x_hi[s])
                part(bank["q"], "q", l, 0, x_lo[s], stop=True).then_inc(s_qkv[s], 1)
                yield
                product(bank["v"], "v", l, x_hi[s], x_lo[s], start=True, stop=True).then_inc(s_qkv[s], 1)
                yield

            def sums(it, s, l):
                pe.wait_ge(s_elu[s], it * (2 * LAYERS) + 2 * l + 1)
                pe.matmul(banks[s][3][:], head_sum[:], kf[s][:], start=True, stop=True).then_inc(s_sum[s], 1)
                yield
                pe.wait_ge(s_kv[s], it * LAYERS + l + 1)
                pe.matmul(banks[s][1][:], head_sum[:], kv[s][:], start=True, stop=True).then_inc(s_sum[s], 1)
                yield

            def mix(it, s, l):
                pe.wait_ge(s_elu[s], it * (2 * LAYERS) + 2 * l + 2)
                product(banks[s][0], "res1", l, x_hi[s], x_lo[s], start=True, stop=False)
                yield
                pe.wait_ge(s_cx[s], it * LAYERS + l + 1)
                pe.matmul(banks[s][0][:], wos[:, l, :], cx[s][:], start=False, stop=True).then_inc(s_z[s], 1)
                yield

            def var(it, s, n, b):
                pe.wait_ge(s_sq[s], it * PER_Y + n + 1)
                pe.matmul(banks[s][b][:], mean_all[:], sq[s][:], start=True, stop=True).then_inc(s_var[s], 1)
                yield

            def up(it, s, l):
                n = it * (2 * LAYERS) + 2 * l + 2
                c = [slice(j * P, (j + 1) * P) for j in range(FB)]
                b = [banks[s][i] for i in (3, 1, 2, 0)]
                pe.wait_ge(s_hi[s], n)
                part(b[0], "up", l, 0, n1_hi[s], start=True, c=c[0])
                part(b[0], "up", l, 1, n1_hi[s], c=c[0])
                part(b[1], "up", l, 0, n1_hi[s], start=True, c=c[1])
                yield
                pe.wait_ge(s_lo[s], n)
                part(b[0], "up", l, 0, n1_lo[s], stop=True, c=c[0]).then_inc(s_h[s], 1)
                yield
                part(b[1], "up", l, 1, n1_hi[s], c=c[1])
                part(b[1], "up", l, 0, n1_lo[s], stop=True, c=c[1]).then_inc(s_h[s], 1)
                yield
                for j in range(2, FB):
                    product(b[j], "up", l, n1_hi[s], n1_lo[s], start=True, stop=True, c=c[j]).then_inc(s_h[s], 1)
                    yield

            def down(it, s, l):
                for j in range(FB):
                    pe.wait_ge(s_relu[s], it * (FB * LAYERS) + FB * l + j + 1)
                    if j == 0:
                        product(banks[s][3], "res2", l, n1_hi[s], n1_lo[s], start=True, stop=False)
                    mm = pe.matmul(banks[s][3][:], w2s[:, l, j, :], hid[s][:, j, :], start=False, stop=j == FB - 1)
                    if j < FB - 1:
                        yield
                mm.then_inc(s_z[s], 1)
                yield

            def centre_(it, s):
                pe.wait_ge(s_y[s], it * PER_Y + 2 * LAYERS)
                pe.matmul(banks[s][0][:], res3[:], x[s][:], start=True, stop=True).then_inc(s_z[s], 1)
                yield

            def gates(it, s):
                pe.wait_ge(s_y[s], it * PER_Y + PER_Y)
                for b, w in enumerate((gates_w, gqs, gks, ggs)):
                    pe.matmul(banks[s][b][:], w[:], hid[s][:, 0, :], start=True, stop=True).then_inc(g_proj[s], 1)
                    yield

            def values(it, s):
                pe.wait_ge(g_act[s], it * NG_ACT + 1)
                pe.wait_ge(g_dve[s], it * NG_DVE + 1)
                for q in range(SEQS):
                    mm = pe.matmul(banks[s][0][:, q * S:(q + 1) * S], hid[s][:, 0, q * S:(q + 1) * S], gvs[:],
                                   start=True, stop=True)
                mm.then_inc(g_proj[s], 1)
                yield

            def scores(it, s):
                pe.wait_ge(g_dve[s], it * NG_DVE + 12)
                pe.wait_ge(g_act[s], it * NG_ACT + 7)
                for h in range(GH):
                    r = slice(32 * h, 32 * h + 32)
                    for q in range(SEQS):
                        c = slice(q * S, (q + 1) * S)
                        mm = pe.matmul(banks[s][h][:, c], K[s][r, c], Q[s][r, c], start=True, stop=True)
                    mm.then_inc(g_score[s], 1)
                    yield

            def outs(it, s):
                for h in range(GH):
                    pe.wait_ge(g_mask[s], it * GH + h + 1)
                    for q in range(SEQS):
                        mm = pe.matmul(banks[s][0][32 * h:32 * h + 32, q * S:(q + 1) * S],
                                       V[s][:, q * S + 32 * h:q * S + 32 * h + 32],
                                       hid[s][:, h, q * S:(q + 1) * S], start=True, stop=True)
                    if h < GH - 1:
                        yield
                mm.then_inc(g_o[s], 1)
                yield

            def ovar(it, s):
                pe.wait_ge(g_act[s], it * NG_ACT + 10)
                pe.matmul(banks[s][1][:], mean_v[:], sq[s][:], start=True, stop=True).then_inc(g_o[s], 1)
                yield

            def project(it, s):
                pe.wait_ge(g_hT[s], it + 1)
                pe.wait_ge(g_gated[s], it + 1)
                for q in range(SEQS):
                    c = slice(q * S, (q + 1) * S)
                    o = banks[s][2 + q // 2][:, (q % 2) * (D + E):(q % 2 + 1) * (D + E)]
                    pe.matmul(o, hT[s][:, c], res_w[:], start=True, stop=False)
                    mm = pe.matmul(o, cx[s][:, c], out_w[:], start=False, stop=True)
                mm.then_inc(g_h2[s], 1)
                yield

            def route(it, s):
                pe.wait_ge(r_dve[s], it * R_DVE + 11)
                o = ohb[s][:].rearrange("p q e -> p (q e)")
                pe.matmul(banks[s][1][:, 0:SEQS * E], tri[:], o, start=True, stop=True)
                pe.matmul(banks[s][1][:, SEQS * E:2 * SEQS * E], ones_b[:], o, start=True, stop=True) \
                    .then_inc(r_cnt[s], 1)
                yield

            def stage(it, s, name):
                if name == "embed":
                    yield from embed(it, s)
                elif name == "centre":
                    yield from centre_(it, s)
                elif name == "cvar":
                    yield from var(it, s, 2 * LAYERS, 2)
                elif name == "gates":
                    yield from gates(it, s)
                elif name == "values":
                    yield from values(it, s)
                elif name == "scores":
                    yield from scores(it, s)
                elif name == "outs":
                    yield from outs(it, s)
                elif name == "ovar":
                    yield from ovar(it, s)
                elif name == "project":
                    yield from project(it, s)
                elif name == "route":
                    yield from route(it, s)
                elif name[0] == "qkv":
                    yield from qkv(it, s, name[1])
                elif name[0] == "sums":
                    yield from sums(it, s, name[1])
                elif name[0] == "mix":
                    yield from mix(it, s, name[1])
                elif name[0] == "var1":
                    yield from var(it, s, 2 * name[1], 2)
                elif name[0] == "up":
                    yield from up(it, s, name[1])
                elif name[0] == "down":
                    yield from down(it, s, name[1])
                elif name[0] == "var2":
                    yield from var(it, s, 2 * name[1] + 1, 1)

            take_turns("pe", stage, 0, None)
            with pe.Fori(0, PAIRS - 1) as j:
                take_turns("pe", stage, j + 1, j)
            take_turns("pe", stage, None, PAIRS - 1)

            def expert_chunk(e, c, cc):
                pe.wait_ge(f_xf, e * CHUNKS + c + 1)
                pe.transpose(ftr[cc % 4][:, 0:P], xfn[cc % 4][:, 0:P], ident[:]).then_inc(f_tr, 1)

            def expert_product(e, c, cc):
                pe.wait_ge(f_xT, e * CHUNKS + c + 1)
                pe.wait_ge(f_o, e * CHUNKS + c + 1)
                o = fyb[cc % 4][:, 0:P]
                pe.matmul(o, xfT[cc % 4][:, 0:P], ews[:, bass.ds(e, 1), :].rearrange("p a d -> p (a d)"),
                          start=True, stop=False)
                pe.matmul(o, ones_r[:], ebs[0:1, bass.ds(e, 1), :].rearrange("p a d -> p (a d)"),
                          start=False, stop=True).then_inc(f_y, 1)

            pe.wait_ge(load_e, 16 * 2)
            with pe.Fori(0, E // 2) as e2:
                for i in range(2 * CHUNKS + 1):
                    if i < 2 * CHUNKS:
                        expert_chunk(e2 * 2 + i // CHUNKS, i % CHUNKS, i)
                    if i >= 1:
                        expert_product(e2 * 2 + (i - 1) // CHUNKS, (i - 1) % CHUNKS, i - 1)


        @block.scalar
        def _(act):
            act.preload_act_table_set("natural_log_exp_and_others")
            act.wait_ge(load_w, 16 * WLOADS)
            act.wait_ge(prep_mean, 2)
            for l in range(LAYERS):
                for j in range(FB):
                    k = l * (FB + 1) + 1 + j
                    last = act.activation(w2s[:, l, j, :], w2s[:, l, j, :], ACT.Identity, bias=wmean[:, k:k + 1])
            last.then_inc(prep_act, 1)
            whole = {"q": wqs, "k": wks, "v": wvs, "up": w1s, "res1": res1, "res2": res2}
            for l in range(LAYERS):
                act.wait_ge(prep_gain, l + 1)
                for n, w in whole.items():
                    last = act.activation(split_w[n][0][:, l, :], w[:, l, :], ACT.Copy)
                last.then_inc(prep_act, 1)
            act.wait_ge(ready, 1)

            def qkv(it, s, l):
                act.wait_ge(s_qkv[s], it * (3 * LAYERS) + 3 * l + 1)
                act.activation(ek[s][:], banks[s][1][:], ACT.Exp, bias=zcol[:, 2, l:l + 1]).then_inc(s_exp[s], 1)
                yield
                act.wait_ge(s_qkv[s], it * (3 * LAYERS) + 3 * l + 2)
                act.activation(eq[s][:], banks[s][0][:], ACT.Exp, bias=zcol[:, 0, l:l + 1]).then_inc(s_exp[s], 1)
                yield

            def sums(it, s, l):
                act.wait_ge(s_tu[s], it * (2 * LAYERS) + 2 * l + 1)
                act.activation(t[s][:], t[s][:], ACT.Ln, bias=eps_attn[:]).then_inc(s_rcp[s], 1)
                yield
                act.wait_ge(s_rcp[s], it * (2 * LAYERS) + 2 * l + 1)
                act.activation(t[s][:], t[s][:], ACT.Exp, scale=-1.0).then_inc(s_rcp[s], 1)
                yield

            def up(it, s, l):
                for j, b in enumerate((3, 1, 2, 0)):
                    act.wait_ge(s_h[s], it * (FB * LAYERS) + FB * l + j + 1)
                    act.activation(hid[s][:, j, :], banks[s][b][:], ACT.Relu, bias=zb1[:, l, j:j + 1]) \
                        .then_inc(s_relu[s], 1)
                    yield

            def residual(it, s):
                i = (LAYERS - 1) * NV
                g, b = i + VEC.index("ln2_g"), i + VEC.index("ln2_b")
                act.wait_ge(s_y[s], it * PER_Y + 2 * LAYERS)
                act.activation(hT[s][:], x[s][:], ACT.Identity, bias=vecs[:, b:b + 1], scale=vecs[:, g:g + 1]) \
                    .then_inc(g_hT[s], 1)
                yield

            def square(it, s, n, b, shift):
                act.wait_ge(s_z[s], it * PER_Y + n + 1)
                act.activation(sq[s][:], banks[s][b][:], ACT.Square, bias=shift).then_inc(s_sq[s], 1)
                yield

            def deviation(it, s, n, b, eps):
                act.wait_ge(s_var[s], it * PER_Y + n + 1)
                act.activation(rs[s][:], banks[s][b][:], ACT.Ln, bias=eps[:]).then_inc(s_rs[s], 1)
                yield
                act.wait_ge(s_rs[s], it * (2 * PER_Y) + 2 * n + 1)
                act.activation(rs[s][:], rs[s][:], ACT.Exp, scale=-0.5).then_inc(s_rs[s], 1)
                yield

            def gates(it, s):
                act.wait_ge(g_proj[s], it * 5 + 1)
                act.activation(lsp[s][:], banks[s][0][:], ACT.Abs, bias=gbs[:]).then_inc(g_act[s], 1)
                yield
                act.wait_ge(g_act[s], it * NG_ACT + 1)
                act.activation(lsp[s][:], lsp[s][:], ACT.Exp, scale=-1.0).then_inc(g_act[s], 1)
                yield
                act.wait_ge(g_act[s], it * NG_ACT + 2)
                act.activation(lsp[s][:], lsp[s][:], ACT.Ln, bias=one_c[:]).then_inc(g_act[s], 1)
                yield
                act.wait_ge(g_dve[s], it * NG_DVE + 2)
                act.activation(hid[s][:, 1, :], hid[s][:, 2, :], ACT.Exp, scale=-1.0).then_inc(g_act[s], 1)
                yield
                act.wait_ge(g_act[s], it * NG_ACT + 4)
                act.activation(hid[s][:, 1, :], hid[s][:, 1, :], ACT.Ln, bias=one_c[:]).then_inc(g_act[s], 1)
                yield
                act.wait_ge(g_act[s], it * NG_ACT + 5)
                act.activation(hid[s][:, 1, :], hid[s][:, 1, :], ACT.Exp, scale=-1.0).then_inc(g_act[s], 1)
                yield

            def values(it, s):
                act.wait_ge(g_proj[s], it * 5 + 5)
                act.wait_ge(g_dve[s], it * NG_DVE + 3)
                act.activation(V[s][:], banks[s][0][:], ACT.Copy).then_inc(g_act[s], 1)
                yield

            def decay(it, s):
                act.wait_ge(g_dve[s], it * NG_DVE + 8)
                act.activation(eQ[s][:], dG[s][:], ACT.Exp, scale=1.0 / 16).then_inc(g_act[s], 1)
                yield
                act.activation(eK[s][:], dG[s][:], ACT.Exp, scale=-1.0 / 16).then_inc(g_act[s], 1)
                yield

            def outs(it, s):
                act.wait_ge(g_o[s], it * 2 + 1)
                act.activation(sq[s][:], banks[s][0][:], ACT.Square).then_inc(g_act[s], 1)
                yield

            def ovar(it, s):
                act.wait_ge(g_o[s], it * 2 + 2)
                act.activation(rs[s][:], banks[s][1][:], ACT.Ln, bias=eps_norm[:]).then_inc(g_act[s], 1)
                yield
                act.wait_ge(g_act[s], it * NG_ACT + 11)
                act.activation(rs[s][:], rs[s][:], ACT.Exp, scale=-0.5).then_inc(g_act[s], 1)
                yield

            def project(it, s):
                act.wait_ge(g_h2[s], it + 1)
                act.wait_ge(row_free[s], it + 1)
                for i in range(2):
                    last = act.activation(row[s][:, 2 * i:2 * i + 2, 0:D],
                                          banks[s][2 + i][:, 0:2 * (D + E)].rearrange("p (q d) -> p q d", q=2)[:, :, 0:D],
                                          ACT.Copy)
                last.then_inc(r_act[s], 1)
                yield

            def stats(it, s):
                act.wait_ge(r_dve[s], it * R_DVE + 2)
                act.activation(lnv[s][:], mv[s][:, :, 1], ACT.Ln, bias=eps_norm[:]).then_inc(r_act[s], 1)
                yield
                act.wait_ge(r_act[s], it * R_ACT + 2)
                act.activation(row[s][:, :, D + 1], lnv[s][:], ACT.Exp, scale=-0.5).then_inc(r_act[s], 1)
                yield

            def route(it, s):
                act.wait_ge(r_dve[s], it * R_DVE + 6)
                act.activation(ex[s][:], lgm[s][:], ACT.Exp).then_inc(r_act[s], 1)
                yield

            def slots(it, s):
                act.wait_ge(r_dve[s], it * R_DVE + 17)
                act.wait_ge(plain_free[s], it + 1)
                for q in range(SEQS):
                    act.activation(plain[s][:, q, :], row[s][:, q, 0:D], ACT.Identity, bias=sc3[s][:, q:q + 1],
                                   scale=sc2[s][:, q:q + 1]).then_inc(r_act[s], 1)
                    yield

            def stage(it, s, name):
                if name == "centre":
                    yield from residual(it, s)
                    yield from square(it, s, 2 * LAYERS, 0, zcen[:])
                elif name == "cvar":
                    yield from deviation(it, s, 2 * LAYERS, 2, eps_norm)
                elif name == "gates":
                    yield from gates(it, s)
                elif name == "values":
                    yield from values(it, s)
                elif name == "decay":
                    yield from decay(it, s)
                elif name == "outs":
                    yield from outs(it, s)
                elif name == "ovar":
                    yield from ovar(it, s)
                elif name == "project":
                    yield from project(it, s)
                elif name == "stats":
                    yield from stats(it, s)
                elif name == "route":
                    yield from route(it, s)
                elif name == "slots":
                    yield from slots(it, s)
                elif name[0] == "qkv":
                    yield from qkv(it, s, name[1])
                elif name[0] == "sums":
                    yield from sums(it, s, name[1])
                elif name[0] == "mix":
                    yield from square(it, s, 2 * name[1], 0, zmix[:, name[1]:name[1] + 1])
                elif name[0] == "var1":
                    yield from deviation(it, s, 2 * name[1], 2, eps_tower)
                elif name[0] == "up":
                    yield from up(it, s, name[1])
                elif name[0] == "down":
                    yield from square(it, s, 2 * name[1] + 1, 3, zdown[:, name[1]:name[1] + 1])
                elif name[0] == "var2":
                    yield from deviation(it, s, 2 * name[1] + 1, 1, eps_tower)

            take_turns("act", stage, 0, None)
            with act.Fori(0, PAIRS - 1) as j:
                take_turns("act", stage, j + 1, j)
            take_turns("act", stage, None, PAIRS - 1)

            with act.Fori(0, E // 2) as e2:
                for i in range(2 * CHUNKS):
                    act.wait_ge(f_tr, e2 * (2 * CHUNKS) + i + 1)
                    act.activation(xfT[i % 4][:, 0:P], ftr[i % 4][:, 0:P], ACT.Copy).then_inc(f_xT, 1)

        @block.vector
        def _(dve):
            dve.memset(zero_col[:], 0.0).then_inc(const, 1)
            dve.memset(before[:, 0, :], 0.0)
            dve.memset(id_row[:, B:], 0.0)

            dve.wait_ge(load_ids, 16)
            dve.tensor_scalar(id_wrap[:], ids[:], 0.0, float(VOCAB), ALU.is_lt, ALU.mult)
            dve.tensor_copy(id_float[:], ids[:]).then_inc(prep_ids, 1)
            dve.wait_ge(prep_ids, 1)
            dve.tensor_tensor(id_float[:], id_wrap[:], id_float[:], ALU.add).then_inc(prep_ids, 1)
            dve.wait_ge(prep_ids, 2)
            dve.tensor_scalar(id_row[:, 0:B], id_float[:], 0.0, float(VOCAB - 1), ALU.max, ALU.min) \
                .then_inc(prep_ids, 1)
            dve.wait_ge(prep_ids, 3)

            def token_rows(it, s):
                dve.tensor_copy(idx[s][:], id_row[:, bass.ds(it * (STREAMS * SEQS) + s * SEQS, SEQS)]) \
                    .then_inc(idx_done[s], 1)

            for s in range(STREAMS):
                token_rows(0, s)
            dve.wait_ge(const, 5)
            dve.tensor_scalar(half_i[:], half_i[:], GK, None, ALU.bitwise_and).then_inc(prep_v, 1)
            dve.wait_ge(prep_v, 1)
            dve.tensor_copy(half_f[:], half_i[:]).then_inc(prep_v, 1)
            dve.wait_ge(prep_v, 2)
            for f in range(2):
                a, b = ((-1.0 / GK, 1.0), (1.0 / GK, 0.0))[f]
                dve.tensor_scalar(half_sel[:, f:f + 1], half_f[:], a, b, ALU.mult, ALU.add)
                dve.tensor_scalar(half_scale[:, f:f + 1], half_f[:], a * GK ** -0.5, b * GK ** -0.5, ALU.mult, ALU.add)
            dve.tensor_copy(res_w[:, 0:D], ident[:])
            dve.wait_ge(load_w, 16 * WLOADS)

            def col(l, name):
                i = l * NV + VEC.index(name)
                return vecs[:, i:i + 1]

            for l in range(LAYERS):
                beta = col(l - 1, "ln2_b") if l else zero_col[:]
                dve.tensor_tensor(work[:, l, 0:1], col(l, "bo"), beta, ALU.add)
                last = dve.tensor_tensor(work[:, l, 1:2], col(l, "b2"), col(l, "ln1_b"), ALU.add)
            last.then_inc(prep_dve, 1)
            k = 0
            wm = []
            for l in range(LAYERS):
                wm.append((wos[:, l, :], k))
                k += 1
                for j in range(FB):
                    wm.append((w2s[:, l, j, :], k))
                    k += 1
            for h in range(GH):
                wm.append((gvs[:, h * GV:(h + 1) * GV], k))
                k += 1
            for w, i in wm:
                last = dve.tensor_reduce(wmean[:, i:i + 1], w, AX_X, ALU.add)
            last.then_inc(prep_mean, 1)
            dve.wait_ge(prep_mean, 1)
            dve.tensor_scalar(wmean[:, 0:k - GH], wmean[:, 0:k - GH], -1.0 / D, None, ALU.mult)
            dve.tensor_scalar(wmean[:, k - GH:k], wmean[:, k - GH:k], -1.0 / GV, None, ALU.mult).then_inc(prep_mean, 1)
            dve.wait_ge(prep_pe, 1)
            b0, b1_, b2_, b3 = banks[0]
            dve.tensor_copy(csw[:], b2_[:, 0:E]).then_inc(prep_dve, 1)
            dve.tensor_copy(gates_w[:], b1_[:, 0:P])
            dve.tensor_copy(res_w[:, D:D + E], b2_[:, 0:E])
            dve.tensor_scalar(res3[:], centre[:], col(LAYERS - 1, "ln2_g"), None, ALU.mult)
            dve.wait_ge(prep_mean, 2)
            for w, i in wm:
                if i % (FB + 1) == 0 or i >= k - GH:
                    dve.tensor_scalar(w, w, wmean[:, i:i + 1], None, ALU.add)

            def gain(l):
                dve.wait_ge(prep_pe, l + 2)
                if l:
                    g = col(l - 1, "ln2_g")
                    for w in (wqs, wks, wvs):
                        dve.tensor_scalar(w[:, l, :], w[:, l, :], g, None, ALU.mult)
                    dve.tensor_scalar(res1[:, l, :], centre[:], g, None, ALU.mult)
                else:
                    dve.tensor_copy(res1[:, l, :], centre[:])
                g = col(l, "ln1_g")
                dve.tensor_scalar(w1s[:, l, :], w1s[:, l, :], g, None, ALU.mult)
                dve.tensor_scalar(res2[:, l, :], centre[:], g, None, ALU.mult).then_inc(prep_gain, 1)

            def rest(l):
                b = banks[1][l]
                for i, name in enumerate(("bq", "bk")):
                    dve.tensor_tensor(zcol[:, 2 * i, l:l + 1], b[:, i:i + 1], col(l, name), ALU.add)
                dve.tensor_tensor(zcol[:, 4, l:l + 1], b[:, 2:3], col(l, "bv"), ALU.add)
                dve.tensor_copy(zmix[:, l:l + 1], b[:, 3:4])
                dve.tensor_copy(zdown[:, l:l + 1], b[:, 4:5])
                for j in range(FB):
                    dve.tensor_tensor(zb1[:, l, j:j + 1], b[:, 5 + j:6 + j], col(l, f"b1_{j}"), ALU.add)
                dve.wait_ge(prep_act, l + 2)
                for n, w in (("q", wqs), ("k", wks), ("v", wvs), ("up", w1s), ("res1", res1), ("res2", res2)):
                    last = dve.tensor_tensor(split_w[n][1][:, l, :], w[:, l, :], split_w[n][0][:, l, :].bitcast(F32),
                                             ALU.subtract)
                return last

            gain(0)
            for l in range(LAYERS):
                if l < LAYERS - 1:
                    gain(l + 1)
                last = rest(l)
            dve.tensor_copy(zcen[:], b0[:, 0:1]).then_inc(prep_v, 1)
            dve.wait_ge(prep_v, 3)
            dve.tensor_scalar(zcol[:, 3, :], zcol[:, 2, :], 1.0, None, ALU.add)
            dve.wait_ge(prep_pe, LAYERS + 2)
            dve.tensor_copy(out_w[:, D:D + E], b3[:, 0:E]).then_inc(ready, 1)

            def embed(it, s):
                dve.wait_ge(embT[s], it + 1)
                dve.scalar_tensor_tensor(out=x[s][:].rearrange("p (q t) -> p q t", q=SEQS),
                                         in0=banks[s][0][:].rearrange("p (q t) -> p q t", q=SEQS), scalar=D ** 0.5,
                                         in1=posT[:].unsqueeze(1).to_broadcast([P, SEQS, S]),
                                         op0=ALU.mult, op1=ALU.add).then_inc(x0[s], 1)
                yield
                dve.wait_ge(x0[s], it + 1)
                dve.tensor_copy(x_hi[s][:], x[s][:]).then_inc(s_hi[s], 1)
                yield
                dve.wait_ge(s_hi[s], it * (2 * LAYERS) + 1)
                dve.tensor_tensor(x_lo[s][:], x[s][:], x_hi[s][:].bitcast(F32), ALU.subtract).then_inc(s_lo[s], 1)
                yield

            def qkv(it, s, l):
                n = it * (2 * LAYERS) + 2 * l
                dve.wait_ge(s_exp[s], n + 1)
                dve.tensor_scalar(ek[s][:], ek[s][:], 1.0, None, ALU.min).then_inc(s_min[s], 1)
                yield
                dve.wait_ge(s_min[s], n + 1)
                dve.scalar_tensor_tensor(out=kf[s][:], in0=banks[s][1][:], scalar=zcol[:, 3, l:l + 1], in1=ek[s][:],
                                         op0=ALU.add, op1=ALU.max).then_inc(s_elu[s], 1)
                yield
                dve.wait_ge(s_exp[s], n + 2)
                dve.tensor_scalar(eq[s][:], eq[s][:], 1.0, -1.0, ALU.min, ALU.add).then_inc(s_min[s], 1)
                yield
                dve.wait_ge(s_qkv[s], it * (3 * LAYERS) + 3 * l + 3)
                dve.wait_ge(s_elu[s], n + 1)
                dve.scalar_tensor_tensor(out=kv[s][:], in0=banks[s][2][:], scalar=zcol[:, 4, l:l + 1], in1=kf[s][:],
                                         op0=ALU.add, op1=ALU.mult).then_inc(s_kv[s], 1)
                yield
                dve.wait_ge(s_min[s], n + 2)
                dve.scalar_tensor_tensor(out=qf[s][:], in0=banks[s][0][:], scalar=zcol[:, 0, l:l + 1], in1=eq[s][:],
                                         op0=ALU.add, op1=ALU.max).then_inc(s_elu[s], 1)
                yield

            def sums(it, s, l):
                dve.wait_ge(s_elu[s], it * (2 * LAYERS) + 2 * l + 2)
                dve.wait_ge(s_sum[s], it * (2 * LAYERS) + 2 * l + 1)
                dve.scalar_tensor_tensor(out=t[s][:], in0=qf[s][:], scalar=1.0, in1=banks[s][3][:],
                                         op0=ALU.add, op1=ALU.mult).then_inc(s_tu[s], 1)
                yield
                dve.wait_ge(s_sum[s], it * (2 * LAYERS) + 2 * l + 2)
                dve.scalar_tensor_tensor(out=u[s][:], in0=qf[s][:], scalar=1.0, in1=banks[s][1][:],
                                         op0=ALU.add, op1=ALU.mult).then_inc(s_tu[s], 1)
                yield
                dve.wait_ge(s_tu[s], it * (2 * LAYERS) + 2 * l + 2)
                dve.wait_ge(s_rcp[s], it * (2 * LAYERS) + 2 * l + 2)
                dve.tensor_tensor(cx[s][:], u[s][:], t[s][:], ALU.mult).then_inc(s_cx[s], 1)
                yield

            def normed(it, s, n, b, shift, dst, hi=None, lo=None):
                dve.wait_ge(s_rs[s], it * (2 * PER_Y) + 2 * n + 2)
                dve.scalar_tensor_tensor(out=dst, in0=banks[s][b][:], scalar=shift, in1=rs[s][:],
                                         op0=ALU.add, op1=ALU.mult).then_inc(s_y[s], 1)
                yield
                if hi is not None:
                    dve.wait_ge(s_y[s], it * PER_Y + n + 1)
                    dve.tensor_copy(hi, dst).then_inc(s_hi[s], 1)
                    yield
                    dve.wait_ge(s_hi[s], it * (2 * LAYERS) + n + 2)
                    dve.tensor_tensor(lo, dst, hi.bitcast(F32), ALU.subtract).then_inc(s_lo[s], 1)
                    yield

            def gates(it, s):
                dve.wait_ge(g_proj[s], it * 5 + 1)
                dve.wait_ge(g_act[s], it * NG_ACT + 1)
                dve.tensor_scalar(mn[s][:], banks[s][0][:], gbs[:], 0.0, ALU.add, ALU.min).then_inc(g_dve[s], 1)
                yield
                dve.wait_ge(g_proj[s], it * 5 + 4)
                dve.tensor_scalar(hid[s][:, 2, :], banks[s][3][:], -40.0, None, ALU.max).then_inc(g_dve[s], 1)
                yield
                dve.wait_ge(g_act[s], it * NG_ACT + 3)
                dve.wait_ge(g_dve[s], it * NG_DVE + 1)
                dve.tensor_tensor(lsp[s][:], mn[s][:], lsp[s][:], ALU.subtract).then_inc(g_dve[s], 1)
                yield
                dve.wait_ge(g_dve[s], it * NG_DVE + 3)
                dve.tensor_tensor_scan(G[s][:], restart[:].rearrange("p q t -> p (q t)"), lsp[s][:], 0.0,
                                       ALU.mult, ALU.add).then_inc(g_dve[s], 1)
                yield

            def decay(it, s):
                dve.wait_ge(g_dve[s], it * NG_DVE + 4)
                n = it * NG_DVE
                g3 = G[s][:].rearrange("p (q t) -> p q t", q=SEQS)
                mids = [g3[:, :, f * HALF + HALF // 2 - 1] for f in range(2)]
                dve.tensor_scalar(ref_a[s][:], mids[0], half_sel[:, 0:1], None, ALU.mult).then_inc(g_dve[s], 1)
                yield
                dve.wait_ge(g_dve[s], n + 5)
                dve.scalar_tensor_tensor(out=ref[s][:], in0=mids[1], scalar=half_sel[:, 1:2], in1=ref_a[s][:],
                                         op0=ALU.mult, op1=ALU.add).then_inc(g_dve[s], 1)
                yield
                dve.wait_ge(g_dve[s], n + 6)
                d3 = dG[s][:].rearrange("p (q t) -> p q t", q=SEQS)
                dve.tensor_tensor(d3, g3, ref[s][:].unsqueeze(2).to_broadcast([P, SEQS, S]), ALU.subtract) \
                    .then_inc(g_dve[s], 1)
                yield
                dve.wait_ge(g_dve[s], n + 7)
                dve.tensor_scalar(dG[s][:], dG[s][:], -DECAY_MAX, DECAY_MAX, ALU.max, ALU.min).then_inc(g_dve[s], 1)
                yield
                dve.wait_ge(g_proj[s], it * 5 + 2)
                dve.wait_ge(g_act[s], it * NG_ACT + 8)
                for f in range(2):
                    a = [x_[:].rearrange("p (q f t) -> p f q t", q=SEQS, f=2)[:, f] for x_ in (Q[s], banks[s][1], eQ[s])]
                    dve.scalar_tensor_tensor(out=a[0], in0=a[1], scalar=half_scale[:, f:f + 1], in1=a[2],
                                             op0=ALU.mult, op1=ALU.mult).then_inc(g_dve[s], 1)
                    yield
                dve.wait_ge(g_proj[s], it * 5 + 3)
                dve.wait_ge(g_act[s], it * NG_ACT + 9)
                dve.tensor_tensor(K[s][:], banks[s][2][:], eK[s][:], ALU.mult).then_inc(g_dve[s], 1)
                yield
                dve.wait_ge(g_act[s], it * NG_ACT + 6)
                dve.wait_ge(g_hT[s], it + 1)
                dve.tensor_tensor(gsil[s][:], banks[s][3][:], hid[s][:, 1, :], ALU.mult).then_inc(g_dve[s], 1)
                yield

            def scores(it, s):
                dve.wait_ge(g_score[s], it * GH + 1)
                for h in range(GH):
                    dve.wait_ge(g_score[s], it * GH + h + 1)
                    dve.tensor_tensor(hid[s][:, h, :].rearrange("p (q t) -> p q t", q=SEQS),
                                      banks[s][h][:].rearrange("p (q t) -> p q t", q=SEQS),
                                      causal[:].unsqueeze(1).to_broadcast([P, SEQS, S]), ALU.mult) \
                        .then_inc(g_mask[s], 1)
                    yield

            def ovar(it, s):
                dve.wait_ge(g_act[s], it * NG_ACT + 12)
                dve.tensor_tensor(u[s][:], banks[s][0][:], rs[s][:], ALU.mult).then_inc(g_dve[s], 1)
                yield
                dve.wait_ge(g_dve[s], it * NG_DVE + 13)
                dve.tensor_tensor(cx[s][:], u[s][:], gsil[s][:], ALU.mult).then_inc(g_gated[s], 1)
                yield

            def project(it, s):
                n = it * R_DVE
                dve.wait_ge(r_act[s], it * R_ACT + 1)
                for q in range(SEQS):
                    last = dve.bn_stats(st[s][:, q, :], row[s][:, q, 0:D])
                last.then_inc(r_dve[s], 1)
                yield
                wait_alone(dve, r_dve[s], n + 1)
                for q in range(SEQS):
                    last = dve.bn_aggr(mv[s][:, q, :], st[s][:, q, :])
                last.then_inc(r_dve[s], 1)
                yield

            def bc(a, n=E):
                return a.unsqueeze(2).to_broadcast([P, SEQS, n])

            def stats(it, s):
                n = it * R_DVE
                dve.wait_ge(r_act[s], it * R_ACT + 3)
                for i in range(2):
                    raw = banks[s][2 + i][:, 0:2 * (D + E)].rearrange("p (q d) -> p q d", q=2)[:, :, D:D + E]
                    last = dve.tensor_tensor(lg[s][:, 2 * i:2 * i + 2, :], raw,
                                             row[s][:, 2 * i:2 * i + 2, D + 1:D + 2].to_broadcast([P, 2, E]), ALU.mult)
                last.then_inc(r_dve[s], 1)
                yield
                dve.wait_ge(r_dve[s], n + 3)
                dve.tensor_tensor(lg[s][:], lg[s][:], sbs[:].unsqueeze(1).to_broadcast([P, SEQS, E]), ALU.add) \
                    .then_inc(r_dve[s], 1)
                yield
                dve.wait_ge(r_dve[s], n + 4)
                dve.tensor_reduce(mx[s][:], lg[s][:], AX_X, ALU.max).then_inc(r_dve[s], 1)
                yield
                dve.wait_ge(r_dve[s], n + 5)
                dve.tensor_tensor(lgm[s][:], lg[s][:], bc(mx[s][:]), ALU.subtract).then_inc(r_dve[s], 1)
                yield
                dve.tensor_tensor(cand[s][:], lg[s][:], bc(mx[s][:]), ALU.is_equal).then_inc(r_dve[s], 1)
                yield
                dve.wait_ge(r_dve[s], n + 7)
                dve.tensor_tensor(cand[s][:], cand[s][:], rank[:], ALU.mult).then_inc(r_dve[s], 1)
                yield
                dve.wait_ge(r_dve[s], n + 8)
                dve.tensor_reduce(m2[s][:], cand[s][:], AX_X, ALU.max).then_inc(r_dve[s], 1)
                yield
                dve.wait_ge(r_dve[s], n + 9)
                dve.tensor_tensor(oh[s][:], rank[:], bc(m2[s][:]), ALU.is_equal).then_inc(r_dve[s], 1)
                yield
                dve.tensor_tensor(ohb[s][:], rank[:], bc(m2[s][:]), ALU.is_equal).then_inc(r_dve[s], 1)
                yield

            def route(it, s):
                n = it * R_DVE
                dve.wait_ge(r_act[s], it * R_ACT + 4)
                dve.tensor_reduce(sm[s][:], ex[s][:], AX_X, ALU.add).then_inc(r_dve[s], 1)
                yield
                dve.wait_ge(r_dve[s], n + 12)
                dve.reciprocal(row[s][:, :, D + 2], sm[s][:]).then_inc(r_dve[s], 1)
                yield
                dve.wait_ge(r_dve[s], n + 13)
                dve.tensor_tensor(sc1[s][:], row[s][:, :, D + 1], row[s][:, :, D + 2], ALU.mult).then_inc(r_dve[s], 1)
                yield
                dve.tensor_copy(row[s][:, :, D], mv[s][:, :, 0]).then_inc(r_dve[s], 1)
                yield
                dve.wait_ge(r_dve[s], n + 14)
                dve.tensor_scalar(sc2[s][:], sc1[s][:], 1.0, None, ALU.add).then_inc(r_dve[s], 1)
                yield
                dve.scalar_tensor_tensor(out=sc3[s][:], in0=sc1[s][:], scalar=-1.0, in1=mv[s][:, :, 0],
                                         op0=ALU.mult, op1=ALU.mult).then_inc(r_dve[s], 1)
                yield
                dve.tensor_scalar(row[s][:, :, D + 3], token_no[:], tile_start[s][:], None, ALU.add) \
                    .then_inc(r_dve[s], 1)
                yield
                dve.wait_ge(r_dve[s], n + 18)
                dve.tensor_scalar(tile_start[s][:], tile_start[s][:], float(STREAMS * TILE), None, ALU.add) \
                    .then_inc(r_dve[s], 1)
                yield
                dve.wait_ge(r_cnt[s], it + 1)
                o = s * SEQS
                for q in range(SEQS):
                    dve.tensor_tensor(before[:, o + q + 1, :], before[:, o + q, :],
                                      banks[s][1][:, (SEQS + q) * E:(SEQS + q + 1) * E], ALU.add) \
                        .then_inc(r_before, 1)
                    dve.wait_ge(r_before, it * (R_BEF) + o + q + 1)
                yield

            def slots(it, s):
                m = it * 7
                cnt = banks[s][1][:, 0:SEQS * E].rearrange("p (q e) -> p q e", q=SEQS)
                dve.tensor_tensor(pick[s][:], cnt, before[:, s * SEQS:(s + 1) * SEQS, :], ALU.add) \
                    .then_inc(r_slot[s], 1)
                yield
                dve.wait_ge(r_slot[s], m + 1)
                dve.tensor_tensor(pick[s][:], pick[s][:], oh[s][:], ALU.mult).then_inc(r_slot[s], 1)
                yield
                if s == STREAMS - 1:
                    dve.tensor_copy(before[:, 0, :], before[:, STREAMS * SEQS, :]).then_inc(r_before, 1)
                    dve.wait_ge(r_before, it * R_BEF + R_BEF)
                dve.wait_ge(r_slot[s], m + 2)
                dve.tensor_reduce(place[s][:], pick[s][:], AX_X, ALU.add).then_inc(r_slot[s], 1)
                yield
                dve.tensor_scalar(slot_f[s][:], m2[s][:], -float(SLOTS), float(E * SLOTS - 1), ALU.mult, ALU.add) \
                    .then_inc(r_slot[s], 1)
                yield
                dve.wait_ge(r_slot[s], m + 4)
                dve.tensor_scalar(over[s][:], place[s][:], float(CAP), FAR, ALU.is_gt, ALU.mult).then_inc(r_slot[s], 1)
                yield
                dve.tensor_tensor(slot_f[s][:], slot_f[s][:], place[s][:], ALU.add).then_inc(r_slot[s], 1)
                yield
                dve.wait_ge(r_slot[s], m + 6)
                dve.tensor_tensor(slot[s][:], slot_f[s][:], over[s][:], ALU.add).then_inc(r_slot[s], 1)
                yield

            def stage(it, s, name):
                if name == "embed":
                    yield from embed(it, s)
                    dve.wait_ge(rows_in[s], it * (16 * SEQS) + 16 * SEQS)
                    token_rows(it + 1, s)
                    yield
                elif name == "cvar":
                    yield from normed(it, s, 2 * LAYERS, 0, zcen[:], hid[s][:, 0, :])
                elif name == "gates":
                    yield from gates(it, s)
                elif name == "decay":
                    yield from decay(it, s)
                elif name == "scores":
                    yield from scores(it, s)
                elif name == "ovar":
                    yield from ovar(it, s)
                elif name == "project":
                    yield from project(it, s)
                elif name == "stats":
                    yield from stats(it, s)
                elif name == "route":
                    yield from route(it, s)
                elif name == "slots":
                    yield from slots(it, s)
                elif name[0] == "qkv":
                    yield from qkv(it, s, name[1])
                elif name[0] == "sums":
                    yield from sums(it, s, name[1])
                elif name[0] == "var1":
                    yield from normed(it, s, 2 * name[1], 0, zmix[:, name[1]:name[1] + 1], n1[s][:],
                               n1_hi[s][:], n1_lo[s][:])
                elif name[0] == "var2":
                    yield from normed(it, s, 2 * name[1] + 1, 3, zdown[:, name[1]:name[1] + 1], x[s][:],
                               *((x_hi[s][:], x_lo[s][:]) if name[1] < LAYERS - 1 else ()))

            take_turns("dve", stage, 0, None)
            with dve.Fori(0, PAIRS - 1) as j:
                take_turns("dve", stage, j + 1, j)
            take_turns("dve", stage, None, PAIRS - 1)

            def row_number(e, b):
                dve.tensor_copy(idp[b][:], xin[b][:, :, D + 3]).then_inc(f_id, 1)

            def norm_chunk(e2, i):
                b, c = i // CHUNKS, i % CHUNKS
                if c == 0:
                    dve.wait_ge(f_in[b], e2 * 16 + 16)
                    dve.wait_ge(f_free[b], e2 + 1)
                    row_number(e2, b)
                if i >= 4:
                    dve.wait_ge(f_tr, e2 * (2 * CHUNKS) + i - 3)
                dve.tensor_scalar(xfn[i % 4][:, 0:D], xin[b][:, c, 0:D], xin[b][:, c, D:D + 1],
                                  xin[b][:, c, D + 1:D + 2], ALU.subtract, ALU.mult).then_inc(f_xf, 1)

            def finish_chunk(e2, i):
                b, c = i // CHUNKS, i % CHUNKS
                dve.wait_ge(f_y, e2 * (2 * CHUNKS) + i + 1)
                dve.scalar_tensor_tensor(out=yo[b][:, c, :], in0=fyb[i % 4][:, 0:D], scalar=xin[b][:, c, D + 2:D + 3],
                                         in1=xin[b][:, c, 0:D], op0=ALU.mult, op1=ALU.add).then_inc(f_o, 1)

            with dve.Fori(0, E // 2) as e2:
                for i in range(2 * CHUNKS + 3):
                    if i < 2 * CHUNKS:
                        norm_chunk(e2, i)
                    if i >= 3:
                        finish_chunk(e2, i - 3)


        @block.gpsimd
        def _(pool):
            pool.memset(void_row[:], FAR)
            pool.memset(onesf[:], 1.0).then_inc(const2, 1)
            for a, v in ((ident, 0.0), (mean_all, 1.0 / D), (ones_b, 1.0), (ones_r, 1.0),
                         (eps_attn, 1e-6), (eps_tower, 1e-3), (eps_norm, 1e-5), (one_c, 1.0), (restart, 1.0),
                         (tile_start[0], 0.0), (tile_start[1], float(TILE))):
                last = pool.memset(a[:], v)
            last.then_inc(pool_step, 1)
            pool.wait_ge(pool_step, 1)
            pool.memset(restart[:, :, 0:1], 0.0)
            pool.affine_select(out=ident[:], in_=ident[:], compare_op=ALU.not_equal, fill=1.0, base=0,
                               pattern=[[-1, P]], channel_multiplier=1).then_inc(pool_step, 1)
            pool.affine_select(out=causal[:], in_=onesf[:], compare_op=ALU.is_ge, fill=0.0, base=0,
                               pattern=[[1, P]], channel_multiplier=-1).then_inc(pool_step, 1)
            for m, w in ((head_sum, HEAD), (mean_v, GV)):
                pool.affine_select(out=m[:].rearrange("p (g c) -> p g c", c=w),
                                   in_=onesf[:].rearrange("p (g c) -> p g c", c=w), compare_op=ALU.is_ge, fill=0.0,
                                   base=0, pattern=[[-w, P // w], [0, w]], channel_multiplier=1).then_inc(pool_step, 1)
            pool.wait_ge(pool_step, 5)
            for m, w in ((head_sum, HEAD), (mean_v, GV)):
                pool.affine_select(out=m[:].rearrange("p (g c) -> p g c", c=w),
                                   in_=m[:].rearrange("p (g c) -> p g c", c=w), compare_op=ALU.is_ge, fill=0.0,
                                   base=w - 1, pattern=[[w, P // w], [0, w]], channel_multiplier=-1) \
                    .then_inc(pool_step, 1)
            pool.tensor_copy(tri[:], causal[:]).then_inc(const, 1)
            pool.iota(rank_i[:], [[0, SEQS], [-1, E]], base=E, channel_multiplier=0).then_inc(pool_step, 1)
            pool.iota(token_i[:], [[S, SEQS]], base=0, channel_multiplier=1).then_inc(pool_step, 1)
            pool.iota(half_i[:], [[0, 1]], base=0, channel_multiplier=1).then_inc(pool_step, 1)
            pool.wait_ge(pool_step, 10)
            pool.tensor_scalar(mean_v[:], mean_v[:], 1.0 / GV, None, ALU.mult).then_inc(const, 1)
            pool.tensor_copy(rank[:], rank_i[:])
            pool.tensor_copy(token_no[:], token_i[:]).then_inc(const, 1)
            pool.tensor_tensor(centre[:], ident[:], mean_all[:], ALU.subtract).then_inc(const, 1)

            def gather(it, s):
                wait_alone(pool, idx_done[s], it + 1)
                for q in range(SEQS):
                    pool.indirect_dma_start(rows[s][:, q, :], None, emb, bass.IndirectOffsetOnAxis(
                        ap=idx[s][:, q:q + 1], axis=0), bounds_check=VOCAB - 1, oob_is_err=False) \
                        .then_inc(rows_in[s], 16)

            for s in range(STREAMS):
                gather(0, s)
                pool.sem_inc(row_free[s], 1)
                pool.sem_inc(plain_free[s], 1)
            for b in range(2):
                pool.sem_inc(f_free[b], 1)
            pool.sem_inc(f_o, 4)
            pool.wait_ge(void_out, 16 * E)
            pool.wait_ge(ready, 1)

            def scatter(it, s):
                pool.wait_ge(r_slot[s], it * 7 + 7)
                wait_alone(pool, r_dve[s], it * R_DVE + 19)
                for q in range(SEQS):
                    pool.indirect_dma_start(slots_dram, bass.IndirectOffsetOnAxis(ap=slot[s][:, q:q + 1], axis=0),
                                            row[s][:, q, :], None, bounds_check=E * SLOTS - 1, oob_is_err=False) \
                        .then_inc(row_out[s], 16)
                    yield

            def stage(it, s, name):
                if name == ("up", 0):
                    pool.wait_ge(embT[s], it + 1)
                    gather(it + 1, s)
                    yield
                elif name == "slots":
                    yield from scatter(it, s)

            take_turns("pool", stage, 0, None)
            with pool.Fori(0, PAIRS - 1) as j:
                take_turns("pool", stage, j + 1, j)
            take_turns("pool", stage, None, PAIRS - 1)
            for s in range(STREAMS):
                pool.wait_ge(rows_in[s], 16 * SEQS * (PAIRS + 1))
                pool.wait_ge(plain_out[s], 16 * PAIRS)

            with pool.Fori(0, E // 2) as e2:
                for b in range(2):
                    for c in range(CHUNKS):
                        wait_alone(pool, f_o, e2 * (2 * CHUNKS) + b * CHUNKS + c + 5)
                        pool.indirect_dma_start(out, bass.IndirectOffsetOnAxis(ap=idp[b][:, c:c + 1], axis=0),
                                                yo[b][:, c, :], None, bounds_check=N - 1, oob_is_err=False) \
                            .then_inc(f_out[b], 16)


_VECS = {"bq": "L0_tok_bq", "bk": "L0_tok_bk", "bv": "L0_tok_bv", "bo": "L0_tok_bo", "ln1_g": "L0_tok_ln1_g",
         "ln1_b": "L0_tok_ln1_b", "b2": "L0_tok_b2", "ln2_g": "L0_tok_ln2_g", "ln2_b": "L0_tok_ln2_b"}


def kernel(**inputs):
    import numpy as np
    import concourse.bacc as bacc
    from concourse.bass_utils import run_bass_kernel_spmd as run

    a = {k: np.asarray(v) for k, v in inputs.items()}
    columns = []
    for l in range(LAYERS):
        for name in VEC:
            if name in _VECS:
                columns.append(a[_VECS[name]][l])
            else:
                j = int(name[-1])
                columns.append(a["L0_tok_b1"][l, j * P:(j + 1) * P])
    ins = [
        ("tok", a["x"].T),
        ("emb", a["L0_tok_emb"]),
        ("pos", a["L0_tok_pos_enc"][:S].T),
        ("wq", a["L0_tok_Wq"]), ("wk", a["L0_tok_Wk"]), ("wv", a["L0_tok_Wv"]), ("wo", a["L0_tok_Wo"]),
        ("w1", a["L0_tok_W1"]), ("w2", a["L0_tok_W2"]),
        ("vec", np.stack(columns, axis=1)),
        ("gq", a["L0_attn_Wq"]), ("gk", a["L0_attn_Wk"]), ("gv", a["L0_attn_Wv"]), ("gg", a["L0_attn_Wg"]),
        ("gk1_t", a["L0_attn_Wgk1"].T), ("gk2", a["L0_attn_Wgk2"]), ("gb", a["L0_attn_bgk2"].reshape(-1, 1)),
        ("go", a["L0_attn_Wo"]), ("go_t", a["L0_attn_Wo"].T),
        ("sw", a["L0_ffn_switch_w"].T), ("sb", a["L0_ffn_switch_b"]),
        ("ew", a["L0_ffn_expert_w"].transpose(2, 0, 1)), ("eb", a["L0_ffn_expert_b"].reshape(1, E, D)),
    ]
    nc = bacc.Bacc("TRN2", target_bir_lowering=False, num_devices=1)
    arrays, args = {}, []
    for name, v in ins:
        v = np.ascontiguousarray(v)
        arrays[f"in_{name}"] = v
        args.append(nc.dram_tensor(f"in_{name}", v.shape, mybir.dt.from_np(v.dtype), kind="ExternalInput").ap())
    b = a["x"].shape[0]
    args.append(nc.dram_tensor("out_rows", (b * S, D), F32, kind="ExternalOutput").ap())
    build(nc, *args)
    r = run(nc, [arrays], core_ids=[0])
    return r.results[0]["out_rows"].reshape(b, S, D)
```
